# Optimizing a Trainium2 kernel written in Bass

```python
import numpy as np
import jax
import jax.numpy as jnp

def _softmax(x, axis=-1):
    return jax.nn.softmax(x, axis=axis)

def _gelu(x):
    return jax.nn.gelu(x, approximate=True)

def _silu(x):
    return jax.nn.silu(x)

def _sigmoid(x):
    return jax.nn.sigmoid(x)

def _layernorm(x, axis=-1, eps=1e-05):
    m = jnp.mean(x, axis=axis, keepdims=True)
    v = jnp.var(x, axis=axis, keepdims=True)
    return (x - m) / jnp.sqrt(v + eps)

def _scatter_add(tgt, idx, src, axis=0):
    return tgt.at[idx].add(src)

def _segment_sum(src, seg, n):
    return jax.ops.segment_sum(src, seg, n)
kernel_name = 'mk_prb_d1_jaxref_r4_2f3741'

def setup_inputs(seed: int=0):
    np.random.seed(seed)
    _w = jnp.asarray

    def _L0_attn_setup():
        import jax, jax.numpy as jnp
        import numpy as np
        B, N, C, H = (8, 1024, 256, 16)
        D = C // H
        EPS = 1e-12

        def _l2norm(x):
            n = jnp.sqrt(jnp.sum(x * x, axis=-1, keepdims=True))
            return x / jnp.maximum(n, EPS)
        key = jax.random.key(seed)
        ks = jax.random.split(key, 5)
        return {'x': jax.random.normal(ks[0], (B, N, C), dtype=jnp.float32), 'qkv_w': jax.random.normal(ks[1], (C, 3 * C), dtype=jnp.float32) * 0.02, 'qkv_b': jax.random.normal(ks[2], (3 * C,), dtype=jnp.float32) * 0.02, 'proj_w': jax.random.normal(ks[3], (C, C), dtype=jnp.float32) * 0.02, 'proj_b': jax.random.normal(ks[4], (C,), dtype=jnp.float32) * 0.02}
    _L0_attn_in = _L0_attn_setup()

    def _L0_ffn_setup():
        import jax, jax.numpy as jnp
        import numpy as np
        HIDDEN = 256
        INTER = 1024
        key = jax.random.key(seed)
        k1, k2, k3, k4, k5 = jax.random.split(key, 5)
        hidden_states = jax.random.normal(k1, (4, 512, HIDDEN), dtype=jnp.float32)
        W1 = jax.random.normal(k2, (HIDDEN, INTER), dtype=jnp.float32) * (1.0 / np.sqrt(HIDDEN))
        b1 = jax.random.normal(k3, (INTER,), dtype=jnp.float32) * 0.02
        W2 = jax.random.normal(k4, (INTER, HIDDEN), dtype=jnp.float32) * (1.0 / np.sqrt(INTER))
        b2 = jax.random.normal(k5, (HIDDEN,), dtype=jnp.float32) * 0.02
        return {'hidden_states': hidden_states, 'W1': W1, 'b1': b1, 'W2': W2, 'b2': b2}
    _L0_ffn_in = _L0_ffn_setup()
    _d = {'L0_attn_x': _L0_attn_in['x'], 'L0_attn_qkv_w': _L0_attn_in['qkv_w'], 'L0_attn_qkv_b': _L0_attn_in['qkv_b'], 'L0_attn_proj_w': _L0_attn_in['proj_w'], 'L0_attn_proj_b': _L0_attn_in['proj_b'], 'L0_ffn_W1': _L0_ffn_in['W1'], 'L0_ffn_b1': _L0_ffn_in['b1'], 'L0_ffn_W2': _L0_ffn_in['W2'], 'L0_ffn_b2': _L0_ffn_in['b2']}
    _x0 = _d['L0_attn_x']
    _d['L0_attn_x'] = jax.random.normal(jax.random.fold_in(jax.random.key(seed), 1), (8, 1024, 256), dtype=_x0.dtype)
    del _x0
    return _d

def reference(L0_attn_x, L0_attn_qkv_w, L0_attn_qkv_b, L0_attn_proj_w, L0_attn_proj_b, L0_ffn_W1, L0_ffn_b1, L0_ffn_W2, L0_ffn_b2):

    def _L0_attn_ref(x, qkv_w, qkv_b, proj_w, proj_b):
        import jax, jax.numpy as jnp
        import numpy as np
        B, N, C, H = (8, 1024, 256, 16)
        D = C // H
        EPS = 1e-12

        def _l2norm(x):
            n = jnp.sqrt(jnp.sum(x * x, axis=-1, keepdims=True))
            return x / jnp.maximum(n, EPS)
        b, n, c = x.shape
        qkv = (x @ qkv_w + qkv_b).reshape(b, n, 3, H, D)
        qkv = jnp.transpose(qkv, (2, 0, 3, 1, 4))
        q, k, v = (qkv[0], qkv[1], qkv[2])
        q = _l2norm(q)
        k = _l2norm(k)
        kv = jnp.einsum('bhnd,bhne->bhde', k, v)
        out = jnp.einsum('bhnd,bhde->bhne', q, kv)
        out = jnp.transpose(out, (0, 2, 1, 3)).reshape(b, n, c)
        return out @ proj_w + proj_b

    def _L0_ffn_ref(hidden_states, W1, b1, W2, b2):
        import jax, jax.numpy as jnp
        import numpy as np
        HIDDEN = 256
        INTER = 1024
        h = jax.nn.relu(jnp.einsum('bsh,hi->bsi', hidden_states, W1) + b1)
        return jnp.einsum('bsi,ih->bsh', h, W2) + b2
    x = L0_attn_x
    xn = _layernorm(x, axis=-1)
    x = x + _L0_attn_ref(xn, L0_attn_qkv_w, L0_attn_qkv_b, L0_attn_proj_w, L0_attn_proj_b) + _L0_ffn_ref(xn, L0_ffn_W1, L0_ffn_b1, L0_ffn_W2, L0_ffn_b2)
    return x

_drawn_inputs = setup_inputs


def setup_inputs(seed=0):
    import zlib

    import numpy as np

    out = dict(_drawn_inputs(seed))
    spreads = {}
    factors = {'L0_attn_proj_b': 6.418, 'L0_ffn_b1': 8.0, 'L0_ffn_b2': 6.418}
    for name, (base, spread) in spreads.items():
        noise = np.random.default_rng([zlib.crc32(name.encode()), seed]).standard_normal(out[name].shape)
        drawn = base * np.exp(spread * noise) if base else spread * noise
        out[name] = jnp.asarray(drawn.astype(out[name].dtype))
    for name, factor in factors.items():
        out[name] = (out[name] * factor).astype(out[name].dtype)
    return out
```

```python
from contextlib import ExitStack

import numpy as np

import concourse.bass as bass
import concourse.mybir as mybir

F32, F32R = mybir.dt.float32, mybir.dt.float32r
ACT = mybir.ActivationFunctionType
ALU = mybir.AluOpType
AXIS = mybir.AxisListType

P = 128
BATCHES, TOKENS, C = 8, 1024, 256
HEADS = 16
D = C // HEADS
INTER = 1024
HALF = TOKENS // 2
TILES = HALF // P
KC = C // P
JC = INTER // P
LN_EPS = 1e-5
NORM_EPS = 1e-12
HF_RING = 4
T_AFTER = 5


def build(nc, x, qkv_w, qkv_b, proj_w, proj_b, w1, b1, w2, b2, out):
    x_halves = x.rearrange("b (u p t) c -> (b u) p (t c)", u=2, p=P)
    out_halves = out.rearrange("b (u p t) c -> (b u) p (t c)", u=2, p=P)

    ctx = ExitStack()
    with ctx:
        def sb(name, shape, dtype=F32):
            return ctx.enter_context(nc.sbuf_tensor(name, shape, dtype))

        def bank(name):
            return ctx.enter_context(nc.psum_tensor(name, [P, 512], F32))

        def sem(name):
            return ctx.enter_context(nc.semaphore(name))

        w1_hi, w1_lo = (sb(f"w1_{n}", [P, KC, INTER], F32R) for n in ("hi", "lo"))
        w2_hi, w2_lo = (sb(f"w2_{n}", [P, JC, C], F32R) for n in ("hi", "lo"))
        wqk_hi, wqk_lo = (sb(f"wqk_{n}", [P, KC, 2 * C], F32R) for n in ("hi", "lo"))
        wv_hi, wv_lo = (sb(f"wv_{n}", [P, KC, C], F32R) for n in ("hi", "lo"))
        proj_hi, proj_lo = (sb(f"proj_{n}", [P, KC, C], F32R) for n in ("hi", "lo"))
        bias_qk = sb("bias_qk", [P, 2 * C])
        bias_out = sb("bias_out", [P, C])
        bias_v = sb("bias_v", [P, KC])
        bias_h = sb("bias_h", [P, JC])
        ident = sb("ident", [P, P])
        ones = sb("ones", [P, P], F32R)
        head_mask = sb("head_mask", [P, KC, P])

        x_sb = sb("x_sb", [P, 2, TILES, C])
        y_sb = sb("y_sb", [P, 2, TILES, C])
        out_sb = sb("out_sb", [P, 2, TILES, C])
        xn = sb("xn", [P, TILES, C])
        xn_hi, xn_lo = (sb(f"xn_{n}", [P, 2, TILES, C], F32R) for n in ("hi", "lo"))
        xT_hi, xT_lo = (sb(f"xT_{n}", [P, 2, KC, HALF], F32R) for n in ("hi", "lo"))
        h_f32 = sb("h_f32", [P, HF_RING, HALF])
        h_hi, h_lo = (sb(f"h_{n}", [P, JC, HALF], F32R) for n in ("hi", "lo"))
        qk = sb("qk", [P, TILES, 2 * C])
        qk_sq = sb("qk_sq", [P, 2, 2 * C])
        k_hi, k_lo = (sb(f"k_{n}", [P, TILES, C], F32R) for n in ("hi", "lo"))
        qT_hi, qT_lo = (sb(f"qT_{n}", [P, KC, TOKENS], F32R) for n in ("hi", "lo"))
        k_sum = sb("k_sum", [P, C])
        ks_hi, ks_lo = (sb(f"ks_{n}", [P, C], F32R) for n in ("hi", "lo"))
        g_hi, g_lo = (sb(f"g_{n}", [P, KC, C], F32R) for n in ("hi", "lo"))
        bv_ks = sb("bv_ks", [P, KC, P])
        kv = sb("kv", [P, KC, P])
        kv_hi, kv_lo = (sb(f"kv_{n}", [P, KC, P], F32R) for n in ("hi", "lo"))
        m_hi, m_lo = (sb(f"m_{n}", [P, KC, C], F32R) for n in ("hi", "lo"))
        ln_parts = sb("ln_parts", [P, TILES, 6])
        ln_sum, ln_dif, ln_m2, ln_mean = (sb(f"ln_{n}", [P, TILES]) for n in ("sum", "dif", "m2", "mean"))
        ln_v, ln_sd, ln_y0, ln_e, ln_rstd = (sb(f"ln_{n}", [P, TILES]) for n in ("v", "sd", "y0", "e", "rstd"))
        qk_v, qk_sd, qk_y0, qk_e, qk_rn = (sb(f"qk_{n}", [P, TILES, 2 * HEADS])
                                           for n in ("v", "sd", "y0", "e", "rn"))
        bias_ffn, ones_f32 = k_sum, bv_ks[:, 0, :]
        wqk_raw = qk[:, 0:KC, :]
        w1_raw = h_f32[:].rearrange("p a b -> p (a b)").rearrange("p (k n) -> p k n", k=KC)
        w2_raw = out_sb[:].rearrange("p a t c -> p (a t) c")
        wv_raw, proj_raw = y_sb[:, 1, 0:KC, :], y_sb[:, 1, KC:2 * KC, :]

        t_bank = [bank(f"t_bank{k}") for k in range(KC)]
        w_bank = [bank(f"w_bank{k}") for k in range(2)]
        o_bank = [bank(f"o_bank{k}") for k in range(2)]
        g_bank = bank("g_bank")
        kv_bank = bank("kv_bank")
        ks_all = kv_bank[:, 0:C]
        kv_raw = kv_bank[:, C:2 * C]

        x_loaded = [sem(f"x_loaded{u}") for u in range(2)]
        wqk_loaded, w1_loaded, w2_loaded, wvp_loaded = (sem(f"{n}_loaded") for n in ("wqk", "w1", "w2", "wvp"))
        bias_qk_loaded, bias_h_loaded, bias_v_loaded, bias_o_loaded = (
            sem(f"bias_{n}_loaded") for n in ("qk", "h", "v", "o"))
        stored = [sem(f"stored{u}") for u in range(2)]
        const_set = sem("const_set")
        ones_ready, bias_out_ready = sem("ones_ready"), sem("bias_out_ready")
        wqk_hi_ready, w1_hi_ready, w2_hi_ready = (sem(f"{n}_hi_ready") for n in ("wqk", "w1", "w2"))
        wqk_ready, w1_ready, w2_ready = (sem(f"{n}_ready") for n in ("wqk", "w1", "w2"))
        wvp_hi_ready, wvp_ready = sem("wvp_hi_ready"), sem("wvp_ready")
        ln_parts_done, ln_sums_done, ln_terms_done = (sem(f"ln_{n}_done") for n in ("parts", "sums", "terms"))
        ln_v_done, ln_sd_done, ln_y0_done, ln_e1_done, ln_e2_done, ln_rstd_done = (
            sem(f"ln_{n}_done") for n in ("v", "sd", "y0", "e1", "e2", "rstd"))
        xn_done, xn_hi_done, xn_split_done = sem("xn_done"), sem("xn_hi_done"), sem("xn_split_done")
        y_set = sem("y_set")
        xT_ready, xT_hi_done, xT_lo_done = sem("xT_ready"), sem("xT_hi_done"), sem("xT_lo_done")
        qk_ready, qk_biased, qk_sq_done, qk_ss_done = (sem(f"qk_{n}") for n in ("ready", "biased", "sq_done", "ss_done"))
        qk_v_done, qk_sd_done, qk_y0_done, qk_e1_done, qk_e2_done, qk_rn_done = (
            sem(f"qk_{n}_done") for n in ("v", "sd", "y0", "e1", "e2", "rn"))
        k_done, q_done = sem("k_done"), sem("q_done")
        k_hi_done, k_lo_done, k_sum_step = (sem(n) for n in ("k_hi_done", "k_lo_done", "k_sum_step"))
        ks_hi_done, ks_done = sem("ks_hi_done"), sem("ks_done")
        g_done = sem("g_done")
        qT_ready, qT_hi_done, qT_lo_done = sem("qT_ready"), sem("qT_hi_done"), sem("qT_lo_done")
        h_ready, h_done, h_copied, h_lo_done = sem("h_ready"), sem("h_done"), sem("h_copied"), sem("h_lo_done")
        y_ready, y_done = sem("y_ready"), sem("y_done")
        g_hi_done, g_lo_done, kv_ready, bv_ks_done = (sem(n) for n in ("g_hi_done", "g_lo_done", "kv_ready", "bv_ks_done"))
        kv_sum_done, kv_masked, kv_hi_done, kv_done = (sem(n) for n in ("kv_sum_done", "kv_masked", "kv_hi_done", "kv_done"))
        m_ready, m_hi_done, m_lo_done = sem("m_ready"), sem("m_hi_done"), sem("m_lo_done")
        o_ready, o_done = sem("o_ready"), sem("o_done")

        def wait(eng, semaphore, count):
            if not (isinstance(count, int) and count <= 0):
                eng.wait_ge(semaphore, count)

        def all_batches(eng, body):
            body(0, False)
            with eng.Fori(1, BATCHES - 1) as b:
                body(b, False)
            body(BATCHES - 1, True)

        block = ctx.enter_context(nc.Block())

        @block.sync
        def _(sp):
            sp.dma_start(x_sb[:, 0, :, :], x_halves[0]).then_inc(x_loaded[0], 16)
            sp.dma_start(wqk_raw, qkv_w[:, 0:2 * C].rearrange("(k p) n -> p k n", p=P)).then_inc(wqk_loaded, 16)
            sp.dma_start(w1_raw, w1.rearrange("(k p) n -> p k n", p=P)).then_inc(w1_loaded, 16)
            sp.dma_start(x_sb[:, 1, :, :], x_halves[1]).then_inc(x_loaded[1], 16)
            sp.dma_start(w2_raw, w2.rearrange("(j p) n -> p j n", p=P)).then_inc(w2_loaded, 16)
            sp.dma_start(wv_raw, qkv_w[:, 2 * C:3 * C].rearrange("(k p) n -> p k n", p=P)).then_inc(wvp_loaded, 16)
            sp.dma_start(proj_raw, proj_w.rearrange("(k p) n -> p k n", p=P)).then_inc(wvp_loaded, 16)

            def body(b, last):
                if not last:
                    for u in range(2):
                        wait(sp, xn_done, 2 * b + u + 1)
                        wait(sp, y_set, 2 * b + u + 1)
                        sp.dma_start(x_sb[:, u, :, :].rearrange("p t c -> p (t c)"),
                                     x_halves[2 * b + u + 2]).then_inc(x_loaded[u], 16)
                for u in range(2):
                    wait(sp, o_done, 4 * b + 2 * u + 2)
                    sp.dma_start(out_halves[2 * b + u],
                                 out_sb[:, u, :, :].rearrange("p t c -> p (t c)")).then_inc(stored[u], 16)

            all_batches(sp, body)
            for u in range(2):
                sp.wait_ge(stored[u], 16 * BATCHES)

        @block.gpsimd
        def _(pool):
            def split_xn(s, u):
                wait(pool, g_done, s - 1)
                wait(pool, xn_hi_done, s + 1)
                nc.gpsimd.tensor_tensor(xn_lo[:, u], xn[:], xn_hi[:, u].bitcast(F32),
                                        ALU.subtract).then_inc(xn_split_done, 1)

            def set_y(b, u):
                wait(pool, x_loaded[u], 16 * (b + 1))
                wait(pool, o_done, 4 * b - 2 + 2 * u)
                nc.gpsimd.tensor_tensor(y_sb[:, u], x_sb[:, u],
                                        bias_out[:].unsqueeze(1).to_broadcast([P, TILES, C]),
                                        ALU.add).then_inc(y_set, 1)

            def split_k(s):
                wait(pool, k_hi_done, s + 1)
                wait(pool, g_done, s)
                nc.gpsimd.tensor_tensor(k_lo[:], qk[:, :, C:2 * C], k_hi[:].bitcast(F32),
                                        ALU.subtract).then_inc(k_lo_done, 1)

            def sum_k(s, u):
                k = qk[:, :, C:2 * C]
                wait(pool, k_done, s + 1)
                if u == 0:
                    nc.gpsimd.tensor_tensor(k_sum[:], k[:, 0], k[:, 1], ALU.add).then_inc(k_sum_step, 2)
                    rest = range(2, TILES)
                else:
                    rest = range(TILES)
                for t in rest:
                    wait(pool, k_sum_step, TILES * s + t)
                    nc.gpsimd.tensor_tensor(k_sum[:], k_sum[:], k[:, t], ALU.add).then_inc(k_sum_step, 1)

            def split_k_sum(b):
                wait(pool, kv_ready, b)
                wait(pool, ks_hi_done, b + 1)
                nc.gpsimd.tensor_tensor(ks_lo[:], k_sum[:], ks_hi[:].bitcast(F32),
                                        ALU.subtract).then_inc(ks_done, 1)

            nc.gpsimd.memset(ident[:], 0.0).then_inc(const_set, 1)
            nc.gpsimd.memset(ones_f32, 1.0).then_inc(const_set, 1)
            nc.gpsimd.memset(head_mask[:], 1.0).then_inc(const_set, 1)
            pool.wait_ge(const_set, 3)
            nc.gpsimd.affine_select(out=ident[:], in_=ident[:], compare_op=ALU.not_equal, fill=1.0, base=0,
                                    pattern=[[-1, P]], channel_multiplier=1).then_inc(const_set, 1)
            blocks = head_mask[:].rearrange("p g (n d) -> p (g n) d", d=D)
            heads_of_chunk = P // D
            for g in range(KC):
                part = blocks[:, g * heads_of_chunk:(g + 1) * heads_of_chunk, :]
                pool.wait_ge(const_set, 4 + 2 * g)
                nc.gpsimd.affine_select(out=part, in_=part, compare_op=ALU.is_ge, fill=0.0, base=0,
                                        pattern=[[-D, heads_of_chunk], [0, D]],
                                        channel_multiplier=1).then_inc(const_set, 1)
                pool.wait_ge(const_set, 5 + 2 * g)
                nc.gpsimd.affine_select(out=part, in_=part, compare_op=ALU.is_ge, fill=0.0, base=D - 1,
                                        pattern=[[D, heads_of_chunk], [0, D]],
                                        channel_multiplier=-1).then_inc(const_set, 1)
            pool.wait_ge(bias_o_loaded, 32)
            nc.gpsimd.tensor_tensor(bias_out[:], bias_out[:], bias_ffn[:], ALU.add).then_inc(bias_out_ready, 1)
            split_xn(0, 0)
            pool.wait_ge(bias_out_ready, 1)
            set_y(0, 0)
            pool.wait_ge(wvp_loaded, 32)
            nc.gpsimd.tensor_copy(wv_hi[:], wv_raw).then_inc(wvp_hi_ready, 1)
            nc.gpsimd.tensor_copy(proj_hi[:], proj_raw).then_inc(wvp_hi_ready, 1)
            pool.wait_ge(wvp_hi_ready, 2)
            nc.gpsimd.tensor_tensor(wv_lo[:], wv_raw, wv_hi[:].bitcast(F32), ALU.subtract).then_inc(wvp_ready, 1)
            nc.gpsimd.tensor_tensor(proj_lo[:], proj_raw, proj_hi[:].bitcast(F32),
                                    ALU.subtract).then_inc(wvp_ready, 1)
            split_k(0)
            sum_k(0, 0)
            split_xn(1, 1)
            pool.wait_ge(wvp_ready, 2)
            set_y(0, 1)

            def body(b, last):
                s = 2 * b + 1
                split_k(s)
                sum_k(s, 1)
                split_k_sum(b)
                if not last:
                    split_xn(s + 1, 0)
                    split_k(s + 1)
                    sum_k(s + 1, 0)
                    split_xn(s + 2, 1)
                    set_y(b + 1, 0)
                    set_y(b + 1, 1)

            all_batches(pool, body)

        @block.scalar
        def _(act):
            def copy(to, what):
                return nc.scalar.activation(to, what, ACT.Copy)

            def ln_sqrt(s):
                wait(act, ln_v_done, s + 1)
                nc.scalar.activation(ln_sd[:], ln_v[:], ACT.Sqrt).then_inc(ln_sd_done, 1)

            def xn_high(s, u):
                wait(act, xn_done, s + 1)
                wait(act, g_done, s - 1)
                copy(xn_hi[:, u], xn[:]).then_inc(xn_hi_done, 1)

            def k_sum_high(b):
                wait(act, k_sum_step, 2 * TILES * (b + 1))
                wait(act, kv_ready, b)
                copy(ks_hi[:], k_sum[:]).then_inc(ks_hi_done, 1)

            def xT_high(s, u):
                for k in range(KC):
                    wait(act, xT_ready, KC * s + k + 1)
                    copy(xT_hi[:, u, k, :], t_bank[k][:]).then_inc(xT_hi_done, 1)

            def qk_square(s):
                for t in range(TILES):
                    wait(act, qk_biased, TILES * s + t + 1)
                    wait(act, qk_ss_done, TILES * s + t - 1)
                    nc.scalar.activation(qk_sq[:, t % 2, :], qk[:, t, :], ACT.Square).then_inc(qk_sq_done, 1)

            def qk_sqrt(s):
                wait(act, qk_v_done, s + 1)
                nc.scalar.activation(qk_sd[:], qk_v[:], ACT.Sqrt).then_inc(qk_sd_done, 1)

            def k_high(s):
                wait(act, k_done, s + 1)
                wait(act, g_done, s)
                copy(k_hi[:], qk[:, :, C:2 * C]).then_inc(k_hi_done, 1)

            def h_chunk(s, j):
                wait(act, h_ready, JC * s + j + 1)
                if j == 0:
                    wait(act, y_ready, 2 * s)
                if j % 2 == 0:
                    nc.scalar.activation(h_hi[:, j, :], w_bank[j % 2][:], ACT.Relu, bias=bias_h[:, j:j + 1])
                wait(act, h_lo_done, JC * s + j + 1 - HF_RING)
                nc.scalar.activation(h_f32[:, j % HF_RING, :], w_bank[j % 2][:], ACT.Relu,
                                     bias=bias_h[:, j:j + 1]).then_inc(h_done, 1)

            def qT_high(s, u):
                for k in range(KC):
                    wait(act, qT_ready, KC * s + k + 1)
                    copy(qT_hi[:, k, u * HALF:(u + 1) * HALF], t_bank[k][:]).then_inc(qT_hi_done, 1)

            act.dma_start(bias_qk[:], qkv_b[0:2 * C].partition_broadcast(P)).then_inc(bias_qk_loaded, 16)
            act.dma_start(bias_h[:], b1.rearrange("(j p) -> p j", p=P),
                          allow_slow_non_contiguous=True).then_inc(bias_h_loaded, 16)
            act.dma_start(bias_out[:], proj_b.partition_broadcast(P)).then_inc(bias_o_loaded, 16)
            act.dma_start(bias_ffn[:], b2.partition_broadcast(P)).then_inc(bias_o_loaded, 16)
            act.dma_start(bias_v[:], qkv_b[2 * C:3 * C].rearrange("(k p) -> p k", p=P),
                          allow_slow_non_contiguous=True).then_inc(bias_v_loaded, 16)
            act.wait_ge(wqk_loaded, 16)
            copy(wqk_hi[:], wqk_raw).then_inc(wqk_hi_ready, 1)
            ln_sqrt(0)
            xT_high(0, 0)
            xn_high(0, 0)
            act.wait_ge(w1_loaded, 16)
            copy(w1_hi[:], w1_raw).then_inc(w1_hi_ready, 1)
            qk_square(0)
            act.wait_ge(const_set, 3)
            copy(ones[:], ones_f32).then_inc(ones_ready, 1)
            qk_sqrt(0)
            k_high(0)
            ln_sqrt(1)
            xn_high(1, 1)
            act.wait_ge(w2_loaded, 16)
            copy(w2_hi[:], w2_raw).then_inc(w2_hi_ready, 1)
            act.wait_ge(bias_h_loaded, 16)
            act.wait_ge(bias_v_loaded, 16)

            def half(s, u, last):
                for j in range(JC):
                    h_chunk(s, j)
                    if j == T_AFTER + 1 and not (last and u):
                        xT_high(s + 1, 1 - u)
                qT_high(s, u)

            def body(b, last):
                half(2 * b, 0, last)
                qk_square(2 * b + 1)
                qk_sqrt(2 * b + 1)
                k_high(2 * b + 1)
                k_sum_high(b)
                if not last:
                    ln_sqrt(2 * b + 2)
                    xn_high(2 * b + 2, 0)
                half(2 * b + 1, 1, last)
                wait(act, g_done, 2 * b + 2)
                copy(g_hi[:], g_bank[:].rearrange("p (k n) -> p k n", k=KC)).then_inc(g_hi_done, 1)
                if not last:
                    qk_square(2 * b + 2)
                wait(act, kv_ready, b + 1)
                wait(act, kv_sum_done, b)
                for g in range(KC):
                    done = nc.scalar.activation(bv_ks[:, g, :], ks_all[:, g * P:(g + 1) * P], ACT.Copy,
                                                scale=bias_v[:, g:g + 1])
                done.then_inc(bv_ks_done, 1)
                if not last:
                    qk_sqrt(2 * b + 2)
                    k_high(2 * b + 2)
                wait(act, m_ready, b + 1)
                copy(m_hi[:], w_bank[0][:].rearrange("p (k n) -> p k n", k=KC)).then_inc(m_hi_done, 1)
                if not last:
                    ln_sqrt(2 * b + 3)
                    xn_high(2 * b + 3, 1)

            all_batches(act, body)

        @block.vector
        def _(dve):
            def less(to, whole, high):
                return nc.vector.tensor_tensor(to, whole, high.bitcast(F32), ALU.subtract)

            def rsqrt(s, v, sd, y0, e, to, sd_done, y0_done, e1_done, e2_done, to_done):
                wait(dve, sd_done, s + 1)
                nc.vector.reciprocal(y0, sd).then_inc(y0_done, 1)
                wait(dve, y0_done, s + 1)
                nc.vector.tensor_tensor(e, v, y0, ALU.mult).then_inc(e1_done, 1)
                wait(dve, e1_done, s + 1)
                nc.vector.scalar_tensor_tensor(e, e, -0.5, y0, ALU.mult, ALU.mult).then_inc(e2_done, 1)
                wait(dve, e2_done, s + 1)
                nc.vector.scalar_tensor_tensor(to, e, 1.5, y0, ALU.add, ALU.mult).then_inc(to_done, 1)
                wait(dve, to_done, s + 1)

            def layer_norm(s, b, u):
                wait(dve, x_loaded[u], 16 * (b + 1))
                for t in range(TILES):
                    done = nc.vector.bn_stats(ln_parts[:, t, :], x_sb[:, u, t, :])
                done.then_inc(ln_parts_done, 1)
                wait(dve, ln_parts_done, s + 1)
                even, odd = ln_parts[:, :, 0:3], ln_parts[:, :, 3:6]
                nc.vector.tensor_tensor(ln_sum[:], even[:, :, 1], odd[:, :, 1], ALU.add)
                nc.vector.tensor_tensor(ln_dif[:], even[:, :, 1], odd[:, :, 1], ALU.subtract)
                nc.vector.tensor_tensor(ln_m2[:], even[:, :, 2], odd[:, :, 2], ALU.add).then_inc(ln_sums_done, 1)
                wait(dve, ln_sums_done, s + 1)
                nc.vector.tensor_scalar(ln_mean[:], ln_sum[:], 0.5, None, ALU.mult)
                nc.vector.tensor_scalar(ln_m2[:], ln_m2[:], 1.0 / C, LN_EPS, ALU.mult, ALU.add)
                nc.vector.scalar_tensor_tensor(ln_dif[:], ln_dif[:], 0.25, ln_dif[:], ALU.mult,
                                               ALU.mult).then_inc(ln_terms_done, 1)
                wait(dve, ln_terms_done, s + 1)
                nc.vector.tensor_tensor(ln_v[:], ln_m2[:], ln_dif[:], ALU.add).then_inc(ln_v_done, 1)
                wait(dve, ln_v_done, s + 1)
                rsqrt(s, ln_v[:], ln_sd[:], ln_y0[:], ln_e[:], ln_rstd[:],
                      ln_sd_done, ln_y0_done, ln_e1_done, ln_e2_done, ln_rstd_done)
                wait(dve, xT_ready, KC * s)
                wait(dve, xn_split_done, s)
                for t in range(TILES):
                    done = nc.vector.tensor_scalar(xn[:, t, :], x_sb[:, u, t, :], ln_mean[:, t:t + 1],
                                                   ln_rstd[:, t:t + 1], ALU.subtract, ALU.mult)
                done.then_inc(xn_done, 1)

            def xT_low(s, u):
                for k in range(KC):
                    wait(dve, xT_hi_done, KC * s + k + 1)
                    less(xT_lo[:, u, k, :], t_bank[k][:], xT_hi[:, u, k, :]).then_inc(xT_lo_done, 1)

            def qk_sums(s):
                def sums(t):
                    wait(dve, qk_sq_done, TILES * s + t + 1)
                    nc.vector.tensor_reduce(qk_v[:, t, :], qk_sq[:, t % 2, :].rearrange("p (h d) -> p h d", d=D),
                                            AXIS.X, ALU.add).then_inc(qk_ss_done, 1)

                wait(dve, qT_ready, KC * s)
                wait(dve, k_lo_done, s)
                wait(dve, k_sum_step, TILES * s)
                for t in range(TILES):
                    wait(dve, qk_ready, TILES * s + t + 1)
                    nc.vector.tensor_tensor(qk[:, t, :], w_bank[t % 2][:], bias_qk[:], ALU.add).then_inc(qk_biased, 1)
                    if t:
                        sums(t - 1)
                sums(TILES - 1)

            def qk_normalise(s):
                wait(dve, qk_ss_done, TILES * (s + 1))
                nc.vector.tensor_scalar(qk_v[:], qk_v[:], NORM_EPS * NORM_EPS, None, ALU.max).then_inc(qk_v_done, 1)
                rsqrt(s, qk_v[:], qk_sd[:], qk_y0[:], qk_e[:], qk_rn[:],
                      qk_sd_done, qk_y0_done, qk_e1_done, qk_e2_done, qk_rn_done)
                for n, done in ((1, k_done), (0, q_done)):
                    part = qk[:, :, n * C:(n + 1) * C].rearrange("p t (h d) -> p t h d", d=D)
                    by = qk_rn[:, :, n * HEADS:(n + 1) * HEADS].unsqueeze(3).to_broadcast([P, TILES, HEADS, D])
                    nc.vector.tensor_tensor(part, part, by, ALU.mult).then_inc(done, 1)

            def h_split(s, j):
                wait(dve, h_done, JC * s + j + 1)
                if j % 2:
                    if j == 1:
                        wait(dve, y_ready, 2 * s)
                    nc.vector.tensor_copy(h_hi[:, j, :], h_f32[:, j % HF_RING, :]).then_inc(h_copied, 1)
                    wait(dve, h_copied, JC // 2 * s + j // 2 + 1)
                less(h_lo[:, j, :], h_f32[:, j % HF_RING, :], h_hi[:, j, :]).then_inc(h_lo_done, 1)

            def qT_low(s, u):
                for k in range(KC):
                    wait(dve, qT_hi_done, KC * s + k + 1)
                    less(qT_lo[:, k, u * HALF:(u + 1) * HALF], t_bank[k][:],
                         qT_hi[:, k, u * HALF:(u + 1) * HALF]).then_inc(qT_lo_done, 1)

            def add_ffn(s, u, n):
                wait(dve, y_ready, 2 * s + n + 1)
                wait(dve, y_set, s + 1)
                tiles = y_sb[:, u, 2 * n:2 * n + 2, :].rearrange("p t c -> p (t c)")
                nc.vector.tensor_tensor(tiles, o_bank[n][:], tiles, ALU.add).then_inc(y_done, 1)

            def add_attention(b, n):
                u, pair = n // 2, n % 2
                wait(dve, o_ready, 4 * b + n + 1)
                wait(dve, y_done, 4 * b + n + 1)
                wait(dve, stored[u], 16 * b)
                y = y_sb[:, u, 2 * pair:2 * pair + 2, :].rearrange("p t c -> p (t c)")
                to = out_sb[:, u, 2 * pair:2 * pair + 2, :].rearrange("p t c -> p (t c)")
                nc.vector.tensor_tensor(to, o_bank[pair][:], y, ALU.add).then_inc(o_done, 1)

            layer_norm(0, 0, 0)
            dve.wait_ge(wqk_hi_ready, 1)
            less(wqk_lo[:], wqk_raw, wqk_hi[:]).then_inc(wqk_ready, 1)
            xT_low(0, 0)
            dve.wait_ge(w1_hi_ready, 1)
            less(w1_lo[:], w1_raw, w1_hi[:]).then_inc(w1_ready, 1)
            dve.wait_ge(bias_qk_loaded, 16)
            qk_sums(0)
            qk_normalise(0)
            layer_norm(1, 0, 1)
            dve.wait_ge(w2_hi_ready, 1)
            less(w2_lo[:], w2_raw, w2_hi[:]).then_inc(w2_ready, 1)

            def half(s, u, last):
                for j in range(JC):
                    h_split(s, j)
                    if j == T_AFTER + 1 and not (last and u):
                        xT_low(s + 1, 1 - u)
                qT_low(s, u)

            def body(b, last):
                half(2 * b, 0, last)
                qk_sums(2 * b + 1)
                qk_normalise(2 * b + 1)
                if not last:
                    layer_norm(2 * b + 2, b + 1, 0)
                for n in range(2):
                    add_ffn(2 * b, 0, n)
                half(2 * b + 1, 1, last)
                wait(dve, g_hi_done, b + 1)
                less(g_lo[:], g_bank[:].rearrange("p (k n) -> p k n", k=KC), g_hi[:]).then_inc(g_lo_done, 1)
                if not last:
                    qk_sums(2 * b + 2)
                wait(dve, bv_ks_done, b + 1)
                nc.vector.tensor_tensor(kv[:], kv_raw.rearrange("p (g n) -> p g n", g=KC), bv_ks[:],
                                        ALU.add).then_inc(kv_sum_done, 1)
                wait(dve, kv_sum_done, b + 1)
                nc.vector.tensor_tensor(kv[:], kv[:], head_mask[:], ALU.mult).then_inc(kv_masked, 1)
                wait(dve, kv_masked, b + 1)
                nc.vector.tensor_copy(kv_hi[:], kv[:]).then_inc(kv_hi_done, 1)
                wait(dve, kv_hi_done, b + 1)
                less(kv_lo[:], kv[:], kv_hi[:]).then_inc(kv_done, 1)
                if not last:
                    qk_normalise(2 * b + 2)
                add_ffn(2 * b + 1, 1, 0)
                wait(dve, m_hi_done, b + 1)
                less(m_lo[:], w_bank[0][:].rearrange("p (k n) -> p k n", k=KC), m_hi[:]).then_inc(m_lo_done, 1)
                if not last:
                    layer_norm(2 * b + 3, b + 1, 1)
                add_ffn(2 * b + 1, 1, 1)
                for n in range(4):
                    add_attention(b, n)

            all_batches(dve, body)

        @block.tensor
        def _(pe):
            def product(to, left, right, first=True, last=True, shared=False):
                nc.tensor.matmul(to, left[0], right[0], start=first, stop=False, skip_group_check=shared)
                nc.tensor.matmul(to, left[0], right[1], start=False, stop=False, skip_group_check=shared)
                return nc.tensor.matmul(to, left[1], right[0], start=False, stop=last, skip_group_check=shared)

            def tile(t):
                return slice(t * P, (t + 1) * P)

            def transpose_x(s):
                wait(pe, xn_done, s + 1)
                wait(pe, xT_lo_done, KC * s)
                wait(pe, qT_lo_done, KC * (s - 1))
                for k in range(KC):
                    for t in range(TILES):
                        done = nc.tensor.transpose(t_bank[k][:, tile(t)], xn[:, t, k * P:(k + 1) * P], ident[:])
                    done.then_inc(xT_ready, 1)

            def query_key(s, u):
                wait(pe, xT_hi_done, KC * (s + 1))
                wait(pe, xT_lo_done, KC * (s + 1))
                for t in range(TILES):
                    if t < 2:
                        wait(pe, h_done, JC * s - 1 + t)
                    else:
                        wait(pe, qk_biased, TILES * s + t - 1)
                    for k in range(KC):
                        done = product(w_bank[t % 2][:],
                                       (xT_hi[:, u, k, tile(t)], xT_lo[:, u, k, tile(t)]),
                                       (wqk_hi[:, k, :], wqk_lo[:, k, :]), k == 0, k == KC - 1)
                    done.then_inc(qk_ready, 1)

            def ffn_up(s, batch, u, with_transposes):
                for j in range(JC):
                    if j < 2:
                        wait(pe, qk_biased, TILES * s + 3 + j)
                        if u == 0 and j == 0:
                            wait(pe, m_lo_done, batch)
                    else:
                        wait(pe, h_done, JC * s + j - 1)
                    for k in range(KC):
                        done = product(w_bank[j % 2][:],
                                       (w1_hi[:, k, tile(j)], w1_lo[:, k, tile(j)]),
                                       (xT_hi[:, u, k, :], xT_lo[:, u, k, :]), k == 0, k == KC - 1)
                    done.then_inc(h_ready, 1)
                    if j == T_AFTER and with_transposes:
                        transpose_x(s + 1)

            def gather(s, b, u):
                wait(pe, xn_split_done, s + 1)
                wait(pe, k_hi_done, s + 1)
                wait(pe, k_lo_done, s + 1)
                if u == 0:
                    wait(pe, g_lo_done, b)
                for t in range(TILES):
                    for k in range(KC):
                        done = product(g_bank[:, k * C:(k + 1) * C],
                                       (xn_hi[:, u, t, k * P:(k + 1) * P], xn_lo[:, u, t, k * P:(k + 1) * P]),
                                       (k_hi[:, t, :], k_lo[:, t, :]),
                                       u == 0 and t == 0 and k == 0, u == 1 and t == TILES - 1, shared=True)
                done.then_inc(g_done, 1)

            def transpose_q(s, after_T):
                wait(pe, q_done, s + 1)
                if after_T:
                    wait(pe, xT_lo_done, KC * (s + 2))
                else:
                    wait(pe, qT_lo_done, KC * s)
                for k in range(KC):
                    for t in range(TILES):
                        done = nc.tensor.transpose(t_bank[k][:, tile(t)], qk[:, t, k * P:(k + 1) * P], ident[:])
                    done.then_inc(qT_ready, 1)

            def ffn_down(s, n, bank_read, count):
                wait(pe, bank_read, count)
                for t in (2 * n, 2 * n + 1):
                    for j in range(JC):
                        wait(pe, h_lo_done, JC * s + j + 1)
                        done = product(o_bank[n][:, (t % 2) * C:(t % 2 + 1) * C],
                                       (h_hi[:, j, tile(t)], h_lo[:, j, tile(t)]),
                                       (w2_hi[:, j, :], w2_lo[:, j, :]), j == 0, j == JC - 1)
                done.then_inc(y_ready, 1)

            def key_value(b):
                wait(pe, ks_done, b + 1)
                wait(pe, g_lo_done, b + 1)
                wait(pe, kv_sum_done, b)
                nc.tensor.matmul(ks_all, ones[:], ks_hi[:], start=True, stop=False)
                nc.tensor.matmul(ks_all, ones[:], ks_lo[:], start=False, stop=True)
                for g in range(KC):
                    for k in range(KC):
                        done = product(kv_raw[:, g * P:(g + 1) * P],
                                       (wv_hi[:, k, g * P:(g + 1) * P], wv_lo[:, k, g * P:(g + 1) * P]),
                                       (g_hi[:, k, g * P:(g + 1) * P], g_lo[:, k, g * P:(g + 1) * P]),
                                       k == 0, k == KC - 1)
                done.then_inc(kv_ready, 1)

            def project(b, bank_read, count):
                wait(pe, kv_done, b + 1)
                wait(pe, bank_read, count)
                for g in range(KC):
                    done = product(w_bank[0][:, g * C:(g + 1) * C], (kv_hi[:, g, :], kv_lo[:, g, :]),
                                   (proj_hi[:, g, :], proj_lo[:, g, :]))
                done.then_inc(m_ready, 1)

            def attend(b):
                wait(pe, m_lo_done, b + 1)
                wait(pe, qT_lo_done, KC * (2 * b + 2))
                for n in range(4):
                    if n < 2:
                        wait(pe, y_done, 4 * b + 3 + n)
                    else:
                        wait(pe, o_done, 4 * b + n - 1)
                    for t in (2 * n, 2 * n + 1):
                        for g in range(KC):
                            done = product(o_bank[n % 2][:, (t % 2) * C:(t % 2 + 1) * C],
                                           (qT_hi[:, g, tile(t)], qT_lo[:, g, tile(t)]),
                                           (m_hi[:, g, :], m_lo[:, g, :]), g == 0, g == KC - 1)
                    done.then_inc(o_ready, 1)

            pe.wait_ge(const_set, 4)
            transpose_x(0)
            pe.wait_ge(wqk_ready, 1)
            query_key(0, 0)
            pe.wait_ge(w1_ready, 1)

            def body(b, last):
                first_half, second_half = 2 * b, 2 * b + 1
                ffn_up(first_half, b, 0, True)
                gather(first_half, b, 0)
                transpose_q(first_half, True)
                query_key(second_half, 1)
                if isinstance(b, int) and b == 0:
                    pe.wait_ge(w2_ready, 1)
                for n in range(2):
                    ffn_down(first_half, n, o_done, 4 * b - 1 + n)
                ffn_up(second_half, b, 1, not last)
                gather(second_half, b, 1)
                transpose_q(second_half, not last)
                if not last:
                    query_key(second_half + 1, 0)
                if isinstance(b, int) and b == 0:
                    pe.wait_ge(wvp_ready, 2)
                    pe.wait_ge(ones_ready, 1)
                key_value(b)
                ffn_down(second_half, 0, y_done, 4 * b + 1)
                if last:
                    project(b, h_done, JC * second_half + JC - 1)
                else:
                    project(b, qk_biased, TILES * (second_half + 1) + 3)
                ffn_down(second_half, 1, y_done, 4 * b + 2)
                attend(b)

            all_batches(pe, body)


INPUTS = {"L0_attn_x": "x", "L0_attn_qkv_w": "qkv_w", "L0_attn_qkv_b": "qkv_b", "L0_attn_proj_w": "proj_w",
          "L0_attn_proj_b": "proj_b", "L0_ffn_W1": "w1", "L0_ffn_b1": "b1", "L0_ffn_W2": "w2", "L0_ffn_b2": "b2"}


def kernel(**inputs):
    import concourse.bacc as bacc
    from concourse.bass_utils import run_bass_kernel_spmd

    nc = bacc.Bacc("TRN2", target_bir_lowering=False, num_devices=1)
    arrays, tensors = {}, {}
    for name, short in INPUTS.items():
        arrays[short] = np.ascontiguousarray(inputs[name])
        tensors[short] = nc.dram_tensor(short, arrays[short].shape, mybir.dt.from_np(arrays[short].dtype),
                                        kind="ExternalInput").ap()
    tensors["out"] = nc.dram_tensor("out", arrays["x"].shape, F32, kind="ExternalOutput").ap()
    build(nc, **tensors)
    return run_bass_kernel_spmd(nc, [arrays], core_ids=[0]).results[0]["out"]
```

```python
from contextlib import ExitStack

import numpy as np

import concourse.bass as bass
import concourse.mybir as mybir

F32, F32R = mybir.dt.float32, mybir.dt.float32r
ACT = mybir.ActivationFunctionType
ALU = mybir.AluOpType
AXIS = mybir.AxisListType

P = 128
BATCHES, TOKENS, C = 8, 1024, 256
HEADS = 16
D = C // HEADS
INTER = 1024
HALF = TOKENS // 2
TILES = HALF // P
KC = C // P
JC = INTER // P
LN_EPS = 1e-5
NORM_EPS = 1e-12
HF_RING = 4
T_AFTER = 5


def build(nc, x, qkv_w, qkv_b, proj_w, proj_b, w1, b1, w2, b2, out):
    x_halves = x.rearrange("b (u p t) c -> (b u) p (t c)", u=2, p=P)
    out_halves = out.rearrange("b (u p t) c -> (b u) p (t c)", u=2, p=P)

    ctx = ExitStack()
    with ctx:
        def sb(name, shape, dtype=F32):
            return ctx.enter_context(nc.sbuf_tensor(name, shape, dtype))

        def bank(name):
            return ctx.enter_context(nc.psum_tensor(name, [P, 512], F32))

        def sem(name):
            return ctx.enter_context(nc.semaphore(name))

        w1_hi, w1_lo = (sb(f"w1_{n}", [P, KC, INTER], F32R) for n in ("hi", "lo"))
        w2_hi, w2_lo = (sb(f"w2_{n}", [P, JC, C], F32R) for n in ("hi", "lo"))
        wqk_hi, wqk_lo = (sb(f"wqk_{n}", [P, KC, 2 * C], F32R) for n in ("hi", "lo"))
        wv_hi, wv_lo = (sb(f"wv_{n}", [P, KC, C], F32R) for n in ("hi", "lo"))
        proj_hi, proj_lo = (sb(f"proj_{n}", [P, KC, C], F32R) for n in ("hi", "lo"))
        bias_qk = sb("bias_qk", [P, 2 * C])
        bias_out = sb("bias_out", [P, C])
        bias_v = sb("bias_v", [P, KC])
        bias_h = sb("bias_h", [P, JC])
        ident = sb("ident", [P, P])
        ones = sb("ones", [P, P], F32R)
        head_mask = sb("head_mask", [P, KC, P])

        x_sb = sb("x_sb", [P, 2, TILES, C])
        y_sb = sb("y_sb", [P, 2, TILES, C])
        out_sb = sb("out_sb", [P, 2, TILES, C])
        xn = sb("xn", [P, TILES, C])
        xn_hi, xn_lo = (sb(f"xn_{n}", [P, 2, TILES, C], F32R) for n in ("hi", "lo"))
        xT_hi, xT_lo = (sb(f"xT_{n}", [P, 2, KC, HALF], F32R) for n in ("hi", "lo"))
        h_f32 = sb("h_f32", [P, HF_RING, HALF])
        h_hi, h_lo = (sb(f"h_{n}", [P, JC, HALF], F32R) for n in ("hi", "lo"))
        qk = sb("qk", [P, TILES, 2 * C])
        qk_sq = sb("qk_sq", [P, 2, 2 * C])
        k_hi, k_lo = (sb(f"k_{n}", [P, TILES, C], F32R) for n in ("hi", "lo"))
        qT_hi, qT_lo = (sb(f"qT_{n}", [P, KC, TOKENS], F32R) for n in ("hi", "lo"))
        k_sum = sb("k_sum", [P, C])
        ks_hi, ks_lo = (sb(f"ks_{n}", [P, C], F32R) for n in ("hi", "lo"))
        g_hi, g_lo = (sb(f"g_{n}", [P, KC, C], F32R) for n in ("hi", "lo"))
        bv_ks = sb("bv_ks", [P, KC, P])
        kv = sb("kv", [P, KC, P])
        kv_hi, kv_lo = (sb(f"kv_{n}", [P, KC, P], F32R) for n in ("hi", "lo"))
        m_hi, m_lo = (sb(f"m_{n}", [P, KC, C], F32R) for n in ("hi", "lo"))
        ln_parts = sb("ln_parts", [P, TILES, 6])
        ln_sum, ln_dif, ln_m2, ln_mean = (sb(f"ln_{n}", [P, TILES]) for n in ("sum", "dif", "m2", "mean"))
        ln_v, ln_sd, ln_y0, ln_e, ln_rstd = (sb(f"ln_{n}", [P, TILES]) for n in ("v", "sd", "y0", "e", "rstd"))
        qk_v, qk_sd, qk_y0, qk_e, qk_rn = (sb(f"qk_{n}", [P, TILES, 2 * HEADS])
                                           for n in ("v", "sd", "y0", "e", "rn"))
        unread = sb("unread", [P, 1])
        bias_ffn, ones_f32 = k_sum, bv_ks[:, 0, :]
        wqk_raw = qk[:, 0:KC, :]
        w1_raw = h_f32[:].rearrange("p a b -> p (a b)").rearrange("p (k n) -> p k n", k=KC)
        w2_raw = out_sb[:].rearrange("p a t c -> p (a t) c")
        wv_raw, proj_raw = y_sb[:, 1, 0:KC, :], y_sb[:, 1, KC:2 * KC, :]

        t_bank = [bank(f"t_bank{k}") for k in range(KC)]
        w_bank = [bank(f"w_bank{k}") for k in range(2)]
        o_bank = [bank(f"o_bank{k}") for k in range(2)]
        g_bank = bank("g_bank")
        kv_bank = bank("kv_bank")
        ks_all = kv_bank[:, 0:C]
        kv_raw = kv_bank[:, C:2 * C]

        x_loaded = [sem(f"x_loaded{u}") for u in range(2)]
        wqk_loaded, w1_loaded, w2_loaded, wvp_loaded = (sem(f"{n}_loaded") for n in ("wqk", "w1", "w2", "wvp"))
        bias_qk_loaded, bias_h_loaded, bias_v_loaded, bias_o_loaded = (
            sem(f"bias_{n}_loaded") for n in ("qk", "h", "v", "o"))
        stored = [sem(f"stored{u}") for u in range(2)]
        const_set = sem("const_set")
        ones_ready, bias_out_ready = sem("ones_ready"), sem("bias_out_ready")
        wqk_hi_ready, w1_hi_ready, w2_hi_ready = (sem(f"{n}_hi_ready") for n in ("wqk", "w1", "w2"))
        wqk_ready, w1_ready, w2_ready = (sem(f"{n}_ready") for n in ("wqk", "w1", "w2"))
        wvp_hi_ready, wvp_ready = sem("wvp_hi_ready"), sem("wvp_ready")
        ln_parts_done, ln_sums_done, ln_terms_done = (sem(f"ln_{n}_done") for n in ("parts", "sums", "terms"))
        ln_v_done, ln_sd_done, ln_y0_done, ln_e1_done, ln_e2_done, ln_rstd_done = (
            sem(f"ln_{n}_done") for n in ("v", "sd", "y0", "e1", "e2", "rstd"))
        xn_done, xn_hi_done, xn_split_done = sem("xn_done"), sem("xn_hi_done"), sem("xn_split_done")
        y_set = sem("y_set")
        xT_ready, xT_hi_done, xT_lo_done = sem("xT_ready"), sem("xT_hi_done"), sem("xT_lo_done")
        qk_ready, qk_biased, qk_sq_done, qk_ss_done = (sem(f"qk_{n}") for n in ("ready", "biased", "sq_done", "ss_done"))
        qk_v_done, qk_sd_done, qk_y0_done, qk_e1_done, qk_e2_done, qk_rn_done = (
            sem(f"qk_{n}_done") for n in ("v", "sd", "y0", "e1", "e2", "rn"))
        k_done, q_done = sem("k_done"), sem("q_done")
        k_hi_done, k_lo_done, k_sum_step = (sem(n) for n in ("k_hi_done", "k_lo_done", "k_sum_step"))
        ks_hi_done, ks_done = sem("ks_hi_done"), sem("ks_done")
        g_done = sem("g_done")
        qT_ready, qT_hi_done, qT_lo_done = sem("qT_ready"), sem("qT_hi_done"), sem("qT_lo_done")
        h_ready, h_done, h_hi_done, h_copied, h_lo_done = (
            sem(n) for n in ("h_ready", "h_done", "h_hi_done", "h_copied", "h_lo_done"))
        y_ready = sem("y_ready")
        y_done = sem("y_done")
        g_hi_done, g_lo_done, kv_ready, bv_ks_done = (sem(n) for n in ("g_hi_done", "g_lo_done", "kv_ready", "bv_ks_done"))
        kv_sum_done, kv_masked, kv_hi_done, kv_done = (sem(n) for n in ("kv_sum_done", "kv_masked", "kv_hi_done", "kv_done"))
        m_ready, m_hi_done, m_lo_done = sem("m_ready"), sem("m_hi_done"), sem("m_lo_done")
        o_ready, o_done = sem("o_ready"), sem("o_done")

        def wait(eng, semaphore, count):
            if not (isinstance(count, int) and count <= 0):
                eng.wait_ge(semaphore, count)

        def t_after(first):
            return JC - 1 if first else T_AFTER

        def all_batches(eng, body):
            body(0, False)
            with eng.Fori(1, BATCHES - 1) as b:
                body(b, False)
            body(BATCHES - 1, True)

        block = ctx.enter_context(nc.Block())

        @block.sync
        def _(sp):
            sp.dma_start(x_sb[:, 0, :, :], x_halves[0]).then_inc(x_loaded[0], 16)
            sp.dma_start(wqk_raw, qkv_w[:, 0:2 * C].rearrange("(k p) n -> p k n", p=P)).then_inc(wqk_loaded, 16)
            sp.dma_start(bias_qk[:], qkv_b[0:2 * C].partition_broadcast(P)).then_inc(bias_qk_loaded, 16)
            sp.dma_start(w1_raw, w1.rearrange("(k p) n -> p k n", p=P)).then_inc(w1_loaded, 16)
            sp.dma_start(x_sb[:, 1, :, :], x_halves[1]).then_inc(x_loaded[1], 16)
            sp.dma_start(bias_h[:], b1.rearrange("(j p) -> p j", p=P),
                         allow_slow_non_contiguous=True).then_inc(bias_h_loaded, 16)
            sp.dma_start(w2_raw, w2.rearrange("(j p) n -> p j n", p=P)).then_inc(w2_loaded, 16)
            sp.dma_start(bias_out[:], proj_b.partition_broadcast(P)).then_inc(bias_o_loaded, 16)
            sp.dma_start(bias_ffn[:], b2.partition_broadcast(P)).then_inc(bias_o_loaded, 16)
            sp.dma_start(bias_v[:], qkv_b[2 * C:3 * C].rearrange("(k p) -> p k", p=P),
                         allow_slow_non_contiguous=True).then_inc(bias_v_loaded, 16)
            sp.dma_start(wv_raw, qkv_w[:, 2 * C:3 * C].rearrange("(k p) n -> p k n", p=P)).then_inc(wvp_loaded, 16)
            sp.dma_start(proj_raw, proj_w.rearrange("(k p) n -> p k n", p=P)).then_inc(wvp_loaded, 16)

            def body(b, last):
                if not last:
                    for u in range(2):
                        wait(sp, xn_done, 2 * b + u + 1)
                        wait(sp, y_set, 2 * b + u + 1)
                        sp.dma_start(x_sb[:, u, :, :].rearrange("p t c -> p (t c)"),
                                     x_halves[2 * b + u + 2]).then_inc(x_loaded[u], 16)
                pieces = 2 if last else 1
                tiles = TILES // pieces
                for u in range(2):
                    for n in range(pieces):
                        wait(sp, o_done, 4 * b + 2 * u + 2 // pieces * (n + 1))
                        sp.dma_start(out_halves[2 * b + u][:, n * tiles * C:(n + 1) * tiles * C],
                                     out_sb[:, u, n * tiles:(n + 1) * tiles, :].rearrange("p t c -> p (t c)")
                                     ).then_inc(stored[u], 16)

            all_batches(sp, body)
            for u in range(2):
                sp.wait_ge(stored[u], 16 * (BATCHES + 1))

        @block.gpsimd
        def _(pool):
            def split_xn(s, u):
                wait(pool, g_done, s - 1)
                wait(pool, xn_hi_done, s + 1)
                nc.gpsimd.tensor_tensor(xn_lo[:, u], xn[:], xn_hi[:, u].bitcast(F32),
                                        ALU.subtract).then_inc(xn_split_done, 1)

            def set_y(b, u):
                wait(pool, x_loaded[u], 16 * (b + 1))
                wait(pool, o_done, 4 * b - 2 + 2 * u)
                nc.gpsimd.tensor_tensor(y_sb[:, u], x_sb[:, u],
                                        bias_out[:].unsqueeze(1).to_broadcast([P, TILES, C]),
                                        ALU.add).then_inc(y_set, 1)

            def split_k(s):
                wait(pool, k_hi_done, s + 1)
                wait(pool, g_done, s)
                nc.gpsimd.tensor_tensor(k_lo[:], qk[:, :, C:2 * C], k_hi[:].bitcast(F32),
                                        ALU.subtract).then_inc(k_lo_done, 1)

            def sum_k(s, u):
                k = qk[:, :, C:2 * C]
                wait(pool, k_done, s + 1)
                if u == 0:
                    nc.gpsimd.tensor_tensor(k_sum[:], k[:, 0], k[:, 1], ALU.add).then_inc(k_sum_step, 2)
                    rest = range(2, TILES)
                else:
                    rest = range(TILES)
                for t in rest:
                    wait(pool, k_sum_step, TILES * s + t)
                    nc.gpsimd.tensor_tensor(k_sum[:], k_sum[:], k[:, t], ALU.add).then_inc(k_sum_step, 1)

            def split_k_sum(b):
                wait(pool, kv_ready, b)
                wait(pool, ks_hi_done, b + 1)
                nc.gpsimd.tensor_tensor(ks_lo[:], k_sum[:], ks_hi[:].bitcast(F32),
                                        ALU.subtract).then_inc(ks_done, 1)

            nc.gpsimd.memset(ident[:], 0.0).then_inc(const_set, 1)
            nc.gpsimd.memset(ones_f32, 1.0).then_inc(const_set, 1)
            nc.gpsimd.memset(head_mask[:], 1.0).then_inc(const_set, 1)
            pool.wait_ge(const_set, 3)
            nc.gpsimd.affine_select(out=ident[:], in_=ident[:], compare_op=ALU.not_equal, fill=1.0, base=0,
                                    pattern=[[-1, P]], channel_multiplier=1).then_inc(const_set, 1)
            blocks = head_mask[:].rearrange("p g (n d) -> p (g n) d", d=D)
            heads_of_chunk = P // D
            for g in range(KC):
                part = blocks[:, g * heads_of_chunk:(g + 1) * heads_of_chunk, :]
                pool.wait_ge(const_set, 4 + 2 * g)
                nc.gpsimd.affine_select(out=part, in_=part, compare_op=ALU.is_ge, fill=0.0, base=0,
                                        pattern=[[-D, heads_of_chunk], [0, D]],
                                        channel_multiplier=1).then_inc(const_set, 1)
                pool.wait_ge(const_set, 5 + 2 * g)
                nc.gpsimd.affine_select(out=part, in_=part, compare_op=ALU.is_ge, fill=0.0, base=D - 1,
                                        pattern=[[D, heads_of_chunk], [0, D]],
                                        channel_multiplier=-1).then_inc(const_set, 1)
            pool.wait_ge(w1_hi_ready, 1)
            nc.gpsimd.tensor_tensor(w1_lo[:], w1_raw, w1_hi[:].bitcast(F32), ALU.subtract).then_inc(w1_ready, 1)
            split_xn(0, 0)
            pool.wait_ge(bias_o_loaded, 32)
            nc.gpsimd.tensor_tensor(bias_out[:], bias_out[:], bias_ffn[:], ALU.add).then_inc(bias_out_ready, 1)
            pool.wait_ge(bias_out_ready, 1)
            set_y(0, 0)
            split_k(0)
            sum_k(0, 0)
            pool.wait_ge(w2_hi_ready, 1)
            nc.gpsimd.tensor_tensor(w2_lo[:], w2_raw, w2_hi[:].bitcast(F32), ALU.subtract).then_inc(w2_ready, 1)
            split_xn(1, 1)
            pool.wait_ge(wvp_loaded, 32)
            nc.gpsimd.tensor_copy(wv_hi[:], wv_raw).then_inc(wvp_hi_ready, 1)
            nc.gpsimd.tensor_copy(proj_hi[:], proj_raw).then_inc(wvp_hi_ready, 1)
            pool.wait_ge(wvp_hi_ready, 2)
            nc.gpsimd.tensor_tensor(wv_lo[:], wv_raw, wv_hi[:].bitcast(F32), ALU.subtract).then_inc(wvp_ready, 1)
            nc.gpsimd.tensor_tensor(proj_lo[:], proj_raw, proj_hi[:].bitcast(F32),
                                    ALU.subtract).then_inc(wvp_ready, 1)
            pool.wait_ge(wvp_ready, 2)
            set_y(0, 1)

            def body(b, last):
                s = 2 * b + 1
                split_k(s)
                sum_k(s, 1)
                if not last:
                    split_xn(s + 1, 0)
                split_k_sum(b)
                if not last:
                    split_k(s + 1)
                    sum_k(s + 1, 0)
                    set_y(b + 1, 0)
                    set_y(b + 1, 1)
                    split_xn(s + 2, 1)

            all_batches(pool, body)

        @block.scalar
        def _(act):
            def copy(to, what):
                return nc.scalar.activation(to, what, ACT.Copy)

            def ln_sqrt(s):
                wait(act, ln_v_done, s + 1)
                nc.scalar.activation(ln_sd[:], ln_v[:], ACT.Sqrt).then_inc(ln_sd_done, 1)

            def xn_high(s, u):
                wait(act, xn_done, s + 1)
                wait(act, g_done, s - 1)
                copy(xn_hi[:, u], xn[:]).then_inc(xn_hi_done, 1)

            def k_sum_high(b):
                wait(act, k_sum_step, 2 * TILES * (b + 1))
                wait(act, kv_ready, b)
                copy(ks_hi[:], k_sum[:]).then_inc(ks_hi_done, 1)

            def xT_high(s, u):
                for k in range(KC):
                    wait(act, xT_ready, KC * s + k + 1)
                    copy(xT_hi[:, u, k, :], t_bank[k][:]).then_inc(xT_hi_done, 1)

            def qk_square(s):
                for t in range(TILES):
                    wait(act, qk_biased, TILES * s + t + 1)
                    wait(act, qk_ss_done, TILES * s + t - 1)
                    nc.scalar.activation(qk_sq[:, t % 2, :], qk[:, t, :], ACT.Square).then_inc(qk_sq_done, 1)

            def qk_sqrt(s):
                wait(act, qk_v_done, s + 1)
                nc.scalar.activation(qk_sd[:], qk_v[:], ACT.Sqrt).then_inc(qk_sd_done, 1)

            def k_high(s):
                wait(act, k_done, s + 1)
                wait(act, g_done, s)
                copy(k_hi[:], qk[:, :, C:2 * C]).then_inc(k_hi_done, 1)

            def h_chunk(s, j):
                wait(act, h_ready, JC * s + j + 1)
                if j == 0:
                    wait(act, y_ready, 2 * s)
                wait(act, h_lo_done, JC * s + j + 1 - HF_RING)
                nc.scalar.activation(h_f32[:, j % HF_RING, :], w_bank[j % 2][:], ACT.Relu,
                                     bias=bias_h[:, j:j + 1]).then_inc(h_done, 1)
                if j % 2 == 0:
                    wait(act, h_done, JC * s + j + 1)
                    copy(h_hi[:, j, :], h_f32[:, j % HF_RING, :]).then_inc(h_hi_done, 1)

            def qT_high(s, u):
                for k in range(KC):
                    wait(act, qT_ready, KC * s + k + 1)
                    copy(qT_hi[:, k, u * HALF:(u + 1) * HALF], t_bank[k][:]).then_inc(qT_hi_done, 1)

            act.wait_ge(const_set, 2)
            nc.scalar.activation(unread[:], ones_f32[:, 0:1], ACT.Sqrt)
            act.wait_ge(wqk_loaded, 16)
            copy(wqk_hi[:], wqk_raw).then_inc(wqk_hi_ready, 1)
            ln_sqrt(0)
            copy(ones[:], ones_f32).then_inc(ones_ready, 1)
            xT_high(0, 0)
            act.wait_ge(w1_loaded, 16)
            copy(w1_hi[:], w1_raw).then_inc(w1_hi_ready, 1)
            xn_high(0, 0)
            ln_sqrt(1)
            act.wait_ge(w2_loaded, 16)
            copy(w2_hi[:], w2_raw).then_inc(w2_hi_ready, 1)
            qk_square(0)
            act.wait_ge(bias_h_loaded, 16)
            act.wait_ge(bias_v_loaded, 16)

            def half(s, b, u, last):
                first = isinstance(s, int) and s == 0
                for j in range(JC):
                    h_chunk(s, j)
                    if j == 1 and first:
                        qk_sqrt(0)
                    if j == 3 and first:
                        k_high(0)
                    if j == (JC - 1 if first else 3) and not (last and u):
                        xn_high(s + 1, 1 - u)
                    if j == 4 and u:
                        k_sum_high(b)
                    if j == min(t_after(first) + 1, JC - 1) and not (last and u):
                        xT_high(s + 1, 1 - u)
                qT_high(s, u)

            def body(b, last):
                half(2 * b, b, 0, last)
                qk_square(2 * b + 1)
                qk_sqrt(2 * b + 1)
                k_high(2 * b + 1)
                if not last:
                    ln_sqrt(2 * b + 2)
                half(2 * b + 1, b, 1, last)
                wait(act, g_done, 2 * b + 2)
                copy(g_hi[:], g_bank[:].rearrange("p (k n) -> p k n", k=KC)).then_inc(g_hi_done, 1)
                if not last:
                    qk_square(2 * b + 2)
                wait(act, kv_ready, b + 1)
                wait(act, kv_sum_done, b)
                for g in range(KC):
                    done = nc.scalar.activation(bv_ks[:, g, :], ks_all[:, g * P:(g + 1) * P], ACT.Copy,
                                                scale=bias_v[:, g:g + 1])
                done.then_inc(bv_ks_done, 1)
                if not last:
                    qk_sqrt(2 * b + 2)
                    k_high(2 * b + 2)
                wait(act, m_ready, b + 1)
                copy(m_hi[:], w_bank[0][:].rearrange("p (k n) -> p k n", k=KC)).then_inc(m_hi_done, 1)
                if not last:
                    ln_sqrt(2 * b + 3)

            all_batches(act, body)

        @block.vector
        def _(dve):
            def less(to, whole, high):
                return nc.vector.tensor_tensor(to, whole, high.bitcast(F32), ALU.subtract)

            def rsqrt(s, v, sd, y0, e, to, sd_done, y0_done, e1_done, e2_done, to_done):
                wait(dve, sd_done, s + 1)
                nc.vector.reciprocal(y0, sd).then_inc(y0_done, 1)
                wait(dve, y0_done, s + 1)
                nc.vector.tensor_tensor(e, v, y0, ALU.mult).then_inc(e1_done, 1)
                wait(dve, e1_done, s + 1)
                nc.vector.scalar_tensor_tensor(e, e, -0.5, y0, ALU.mult, ALU.mult).then_inc(e2_done, 1)
                wait(dve, e2_done, s + 1)
                nc.vector.scalar_tensor_tensor(to, e, 1.5, y0, ALU.add, ALU.mult).then_inc(to_done, 1)
                wait(dve, to_done, s + 1)

            def variance(s, b, u):
                wait(dve, x_loaded[u], 16 * (b + 1))
                for t in range(TILES):
                    done = nc.vector.bn_stats(ln_parts[:, t, :], x_sb[:, u, t, :])
                done.then_inc(ln_parts_done, 1)
                wait(dve, ln_parts_done, s + 1)
                even, odd = ln_parts[:, :, 0:3], ln_parts[:, :, 3:6]
                nc.vector.tensor_tensor(ln_sum[:], even[:, :, 1], odd[:, :, 1], ALU.add)
                nc.vector.tensor_tensor(ln_dif[:], even[:, :, 1], odd[:, :, 1], ALU.subtract)
                nc.vector.tensor_tensor(ln_m2[:], even[:, :, 2], odd[:, :, 2], ALU.add).then_inc(ln_sums_done, 1)
                wait(dve, ln_sums_done, s + 1)
                nc.vector.tensor_scalar(ln_mean[:], ln_sum[:], 0.5, None, ALU.mult)
                nc.vector.tensor_scalar(ln_m2[:], ln_m2[:], 1.0 / C, LN_EPS, ALU.mult, ALU.add)
                nc.vector.scalar_tensor_tensor(ln_dif[:], ln_dif[:], 0.25, ln_dif[:], ALU.mult,
                                               ALU.mult).then_inc(ln_terms_done, 1)
                wait(dve, ln_terms_done, s + 1)
                nc.vector.tensor_tensor(ln_v[:], ln_m2[:], ln_dif[:], ALU.add).then_inc(ln_v_done, 1)
                wait(dve, ln_v_done, s + 1)

            def normalise(s, u):
                rsqrt(s, ln_v[:], ln_sd[:], ln_y0[:], ln_e[:], ln_rstd[:],
                      ln_sd_done, ln_y0_done, ln_e1_done, ln_e2_done, ln_rstd_done)
                wait(dve, xT_ready, KC * s)
                wait(dve, xn_split_done, s)
                for t in range(TILES):
                    done = nc.vector.tensor_scalar(xn[:, t, :], x_sb[:, u, t, :], ln_mean[:, t:t + 1],
                                                   ln_rstd[:, t:t + 1], ALU.subtract, ALU.mult)
                done.then_inc(xn_done, 1)

            def xT_low(s, u):
                for k in range(KC):
                    wait(dve, xT_hi_done, KC * s + k + 1)
                    less(xT_lo[:, u, k, :], t_bank[k][:], xT_hi[:, u, k, :]).then_inc(xT_lo_done, 1)

            def qk_sums(s):
                def sums(t):
                    wait(dve, qk_sq_done, TILES * s + t + 1)
                    nc.vector.tensor_reduce(qk_v[:, t, :], qk_sq[:, t % 2, :].rearrange("p (h d) -> p h d", d=D),
                                            AXIS.X, ALU.add).then_inc(qk_ss_done, 1)

                wait(dve, qT_ready, KC * s)
                wait(dve, k_lo_done, s)
                wait(dve, k_sum_step, TILES * s)
                for t in range(TILES):
                    wait(dve, qk_ready, TILES * s + t + 1)
                    nc.vector.tensor_tensor(qk[:, t, :], w_bank[t % 2][:], bias_qk[:], ALU.add).then_inc(qk_biased, 1)
                    if t:
                        sums(t - 1)
                sums(TILES - 1)

            def norms(s):
                wait(dve, qk_ss_done, TILES * (s + 1))
                nc.vector.tensor_scalar(qk_v[:], qk_v[:], NORM_EPS * NORM_EPS, None, ALU.max).then_inc(qk_v_done, 1)
                rsqrt(s, qk_v[:], qk_sd[:], qk_y0[:], qk_e[:], qk_rn[:],
                      qk_sd_done, qk_y0_done, qk_e1_done, qk_e2_done, qk_rn_done)

            def divide(n, done):
                part = qk[:, :, n * C:(n + 1) * C].rearrange("p t (h d) -> p t h d", d=D)
                by = qk_rn[:, :, n * HEADS:(n + 1) * HEADS].unsqueeze(3).to_broadcast([P, TILES, HEADS, D])
                nc.vector.tensor_tensor(part, part, by, ALU.mult).then_inc(done, 1)

            def qk_normalise(s):
                norms(s)
                divide(1, k_done)
                divide(0, q_done)

            def h_split(s, j):
                if j % 2 == 0:
                    wait(dve, h_hi_done, JC // 2 * s + j // 2 + 1)
                else:
                    wait(dve, h_done, JC * s + j + 1)
                    if j == 1:
                        wait(dve, y_ready, 2 * s)
                    nc.vector.tensor_copy(h_hi[:, j, :], h_f32[:, j % HF_RING, :]).then_inc(h_copied, 1)
                    wait(dve, h_copied, JC // 2 * s + j // 2 + 1)
                less(h_lo[:, j, :], h_f32[:, j % HF_RING, :], h_hi[:, j, :]).then_inc(h_lo_done, 1)

            def qT_low(s, u):
                for k in range(KC):
                    wait(dve, qT_hi_done, KC * s + k + 1)
                    less(qT_lo[:, k, u * HALF:(u + 1) * HALF], t_bank[k][:],
                         qT_hi[:, k, u * HALF:(u + 1) * HALF]).then_inc(qT_lo_done, 1)

            def add_ffn(b, n):
                wait(dve, y_ready, 4 * b + n + 1)
                wait(dve, y_set, 2 * b + 1)
                tiles = y_sb[:, 0, 2 * n:2 * n + 2, :].rearrange("p t c -> p (t c)")
                nc.vector.tensor_tensor(tiles, o_bank[n][:], tiles, ALU.add).then_inc(y_done, 1)

            def add_attention(b, n):
                u, pair = n // 2, n % 2
                wait(dve, o_ready, 4 * b + n + 1)
                if u == 0:
                    wait(dve, y_done, 2 * b + n + 1)
                else:
                    wait(dve, y_set, 2 * b + 2)
                wait(dve, stored[u], 16 * b)
                y = y_sb[:, u, 2 * pair:2 * pair + 2, :].rearrange("p t c -> p (t c)")
                to = out_sb[:, u, 2 * pair:2 * pair + 2, :].rearrange("p t c -> p (t c)")
                nc.vector.tensor_tensor(to, (o_bank if u else w_bank)[pair][:], y, ALU.add).then_inc(o_done, 1)

            variance(0, 0, 0)
            normalise(0, 0)
            dve.wait_ge(wqk_hi_ready, 1)
            less(wqk_lo[:], wqk_raw, wqk_hi[:]).then_inc(wqk_ready, 1)
            xT_low(0, 0)
            variance(1, 0, 1)
            dve.wait_ge(bias_qk_loaded, 16)
            qk_sums(0)
            norms(0)
            divide(1, k_done)

            def half(s, u, last):
                first = isinstance(s, int) and s == 0
                for j in range(JC):
                    h_split(s, j)
                    if j == 1 and first:
                        normalise(1, 1)
                    if j == 5 and first:
                        divide(0, q_done)
                    if j == min(t_after(first) + 1, JC - 1) and not (last and u):
                        xT_low(s + 1, 1 - u)

            def body(b, last):
                half(2 * b, 0, last)
                qk_sums(2 * b + 1)
                qT_low(2 * b, 0)
                qk_normalise(2 * b + 1)
                if not last:
                    variance(2 * b + 2, b + 1, 0)
                    normalise(2 * b + 2, 0)
                for n in range(2):
                    add_ffn(b, n)
                half(2 * b + 1, 1, last)
                wait(dve, g_hi_done, b + 1)
                less(g_lo[:], g_bank[:].rearrange("p (k n) -> p k n", k=KC), g_hi[:]).then_inc(g_lo_done, 1)
                if not last:
                    qk_sums(2 * b + 2)
                qT_low(2 * b + 1, 1)
                wait(dve, bv_ks_done, b + 1)
                nc.vector.tensor_tensor(kv[:], kv_raw.rearrange("p (g n) -> p g n", g=KC), bv_ks[:],
                                        ALU.add).then_inc(kv_sum_done, 1)
                wait(dve, kv_sum_done, b + 1)
                nc.vector.tensor_tensor(kv[:], kv[:], head_mask[:], ALU.mult).then_inc(kv_masked, 1)
                wait(dve, kv_masked, b + 1)
                nc.vector.tensor_copy(kv_hi[:], kv[:]).then_inc(kv_hi_done, 1)
                wait(dve, kv_hi_done, b + 1)
                less(kv_lo[:], kv[:], kv_hi[:]).then_inc(kv_done, 1)
                if not last:
                    qk_normalise(2 * b + 2)
                wait(dve, m_hi_done, b + 1)
                less(m_lo[:], w_bank[0][:].rearrange("p (k n) -> p k n", k=KC), m_hi[:]).then_inc(m_lo_done, 1)
                if not last:
                    variance(2 * b + 3, b + 1, 1)
                for n in range(4):
                    add_attention(b, n)
                if not last:
                    normalise(2 * b + 3, 1)

            all_batches(dve, body)

        @block.tensor
        def _(pe):
            def product(to, left, right, first=True, last=True, shared=False):
                nc.tensor.matmul(to, left[0], right[0], start=first, stop=False, skip_group_check=shared)
                nc.tensor.matmul(to, left[0], right[1], start=False, stop=False, skip_group_check=shared)
                return nc.tensor.matmul(to, left[1], right[0], start=False, stop=last, skip_group_check=shared)

            def tile(t):
                return slice(t * P, (t + 1) * P)

            def transpose_x(s):
                wait(pe, xn_done, s + 1)
                wait(pe, xT_lo_done, KC * s)
                wait(pe, qT_lo_done, KC * (s - 1))
                for k in range(KC):
                    for t in range(TILES):
                        done = nc.tensor.transpose(t_bank[k][:, tile(t)], xn[:, t, k * P:(k + 1) * P], ident[:])
                    done.then_inc(xT_ready, 1)

            def query_key(s, u):
                wait(pe, xT_hi_done, KC * (s + 1))
                wait(pe, xT_lo_done, KC * (s + 1))
                for t in range(TILES):
                    if t < 2:
                        wait(pe, h_done, JC * s - 1 + t)
                    else:
                        wait(pe, qk_biased, TILES * s + t - 1)
                    for k in range(KC):
                        done = product(w_bank[t % 2][:],
                                       (xT_hi[:, u, k, tile(t)], xT_lo[:, u, k, tile(t)]),
                                       (wqk_hi[:, k, :], wqk_lo[:, k, :]), k == 0, k == KC - 1)
                    done.then_inc(qk_ready, 1)

            def ffn_up(s, batch, u, with_transposes):
                for j in range(JC):
                    if j < 2:
                        wait(pe, qk_biased, TILES * s + 3 + j)
                        if u == 0:
                            wait(pe, o_done, 4 * batch - 3 + j)
                    else:
                        wait(pe, h_done, JC * s + j - 1)
                    for k in range(KC):
                        done = product(w_bank[j % 2][:],
                                       (w1_hi[:, k, tile(j)], w1_lo[:, k, tile(j)]),
                                       (xT_hi[:, u, k, :], xT_lo[:, u, k, :]), k == 0, k == KC - 1)
                    done.then_inc(h_ready, 1)
                    if j == t_after(isinstance(s, int) and s == 0) and with_transposes:
                        transpose_x(s + 1)

            def gather(s, b, u):
                wait(pe, xn_split_done, s + 1)
                wait(pe, k_hi_done, s + 1)
                wait(pe, k_lo_done, s + 1)
                if u == 0:
                    wait(pe, g_lo_done, b)
                for t in range(TILES):
                    for k in range(KC):
                        done = product(g_bank[:, k * C:(k + 1) * C],
                                       (xn_hi[:, u, t, k * P:(k + 1) * P], xn_lo[:, u, t, k * P:(k + 1) * P]),
                                       (k_hi[:, t, :], k_lo[:, t, :]),
                                       u == 0 and t == 0 and k == 0, u == 1 and t == TILES - 1, shared=True)
                done.then_inc(g_done, 1)

            def transpose_q(s, after_T):
                wait(pe, q_done, s + 1)
                if after_T:
                    wait(pe, xT_lo_done, KC * (s + 2))
                else:
                    wait(pe, qT_lo_done, KC * s)
                for k in range(KC):
                    for t in range(TILES):
                        done = nc.tensor.transpose(t_bank[k][:, tile(t)], qk[:, t, k * P:(k + 1) * P], ident[:])
                    done.then_inc(qT_ready, 1)

            def ffn_down(s, u, t):
                to = o_bank[t // 2][:, (t % 2) * C:(t % 2 + 1) * C]
                for j in range(JC):
                    wait(pe, h_lo_done, JC * s + j + 1)
                    done = product(to, (h_hi[:, j, tile(t)], h_lo[:, j, tile(t)]),
                                   (w2_hi[:, j, :], w2_lo[:, j, :]),
                                   j == 0 and (u == 0 or t % 2 == 0), j == JC - 1 and u == 0, shared=u == 1)
                if t % 2:
                    done.then_inc(y_ready, 1)

            def key_value(b):
                wait(pe, ks_done, b + 1)
                wait(pe, g_lo_done, b + 1)
                wait(pe, kv_sum_done, b)
                nc.tensor.matmul(ks_all, ones[:], ks_hi[:], start=True, stop=False)
                nc.tensor.matmul(ks_all, ones[:], ks_lo[:], start=False, stop=True)
                for g in range(KC):
                    for k in range(KC):
                        done = product(kv_raw[:, g * P:(g + 1) * P],
                                       (wv_hi[:, k, g * P:(g + 1) * P], wv_lo[:, k, g * P:(g + 1) * P]),
                                       (g_hi[:, k, g * P:(g + 1) * P], g_lo[:, k, g * P:(g + 1) * P]),
                                       k == 0, k == KC - 1)
                done.then_inc(kv_ready, 1)

            def project(b, bank_read, count):
                wait(pe, kv_done, b + 1)
                wait(pe, bank_read, count)
                for g in range(KC):
                    done = product(w_bank[0][:, g * C:(g + 1) * C], (kv_hi[:, g, :], kv_lo[:, g, :]),
                                   (proj_hi[:, g, :], proj_lo[:, g, :]))
                done.then_inc(m_ready, 1)

            def attend(b, last):
                wait(pe, m_lo_done, b + 1)
                wait(pe, qT_lo_done, KC * (2 * b + 2))
                for t in range(2 * TILES):
                    second = t >= TILES
                    bank_of = (o_bank if second else w_bank)[t % TILES // 2]
                    if t == 2 and last:
                        wait(pe, h_done, JC * (2 * b + 2))
                    elif t == 2:
                        wait(pe, qk_biased, TILES * (2 * b + 3))
                    for g in range(KC):
                        done = product(bank_of[:, (t % 2) * C:(t % 2 + 1) * C],
                                       (qT_hi[:, g, tile(t)], qT_lo[:, g, tile(t)]),
                                       (m_hi[:, g, :], m_lo[:, g, :]),
                                       g == 0 and not second, g == KC - 1, shared=second)
                    if t % 2:
                        done.then_inc(o_ready, 1)

            def keep_warm(count):
                for _ in range(count):
                    nc.tensor.matmul(kv_bank[:, 0:P], ident[:], ident[:], start=True, stop=True)

            pe.wait_ge(const_set, 4)
            keep_warm(20)
            transpose_x(0)
            keep_warm(7)
            pe.wait_ge(wqk_ready, 1)
            query_key(0, 0)
            pe.wait_ge(w1_ready, 1)

            def body(b, last):
                first_half, second_half = 2 * b, 2 * b + 1
                ffn_up(first_half, b, 0, True)
                gather(first_half, b, 0)
                transpose_q(first_half, True)
                query_key(second_half, 1)
                if isinstance(b, int) and b == 0:
                    pe.wait_ge(w2_ready, 1)
                for t in range(TILES):
                    if t % 2 == 0:
                        wait(pe, o_done, 4 * b - 1 + t // 2)
                    ffn_down(first_half, 0, t)
                ffn_up(second_half, b, 1, not last)
                gather(second_half, b, 1)
                transpose_q(second_half, not last)
                if isinstance(b, int) and b == 0:
                    pe.wait_ge(wvp_ready, 2)
                    pe.wait_ge(ones_ready, 1)
                if not last:
                    query_key(second_half + 1, 0)
                    key_value(b)
                for t in range(TILES):
                    if t % 2 == 0:
                        wait(pe, y_done, 2 * b + t // 2 + 1)
                    ffn_down(second_half, 1, t)
                    if last and t == 1:
                        key_value(b)
                    if last and t == 2:
                        project(b, h_done, JC * second_half + JC - 1)
                    if not last and t == 1:
                        project(b, qk_biased, TILES * (second_half + 1) + 3)
                attend(b, last)

            all_batches(pe, body)


INPUTS = {"L0_attn_x": "x", "L0_attn_qkv_w": "qkv_w", "L0_attn_qkv_b": "qkv_b", "L0_attn_proj_w": "proj_w",
          "L0_attn_proj_b": "proj_b", "L0_ffn_W1": "w1", "L0_ffn_b1": "b1", "L0_ffn_W2": "w2", "L0_ffn_b2": "b2"}


def kernel(**inputs):
    import concourse.bacc as bacc
    from concourse.bass_utils import run_bass_kernel_spmd

    nc = bacc.Bacc("TRN2", target_bir_lowering=False, num_devices=1)
    arrays, tensors = {}, {}
    for name, short in INPUTS.items():
        arrays[short] = np.ascontiguousarray(inputs[name])
        tensors[short] = nc.dram_tensor(short, arrays[short].shape, mybir.dt.from_np(arrays[short].dtype),
                                        kind="ExternalInput").ap()
    tensors["out"] = nc.dram_tensor("out", arrays["x"].shape, F32, kind="ExternalOutput").ap()
    build(nc, **tensors)
    return run_bass_kernel_spmd(nc, [arrays], core_ids=[0]).results[0]["out"]
```

```python
from contextlib import ExitStack

import numpy as np

import concourse.bass as bass
import concourse.mybir as mybir

F32, F32R = mybir.dt.float32, mybir.dt.float32r
ACT = mybir.ActivationFunctionType
ALU = mybir.AluOpType
AXIS = mybir.AxisListType

P = 128
BATCHES, TOKENS, C = 8, 1024, 256
HEADS = 16
D = C // HEADS
INTER = 1024
HALF = TOKENS // 2
TILES = HALF // P
KC = C // P
JC = INTER // P
LN_EPS = 1e-5
NORM_EPS = 1e-12
HF_RING = 4
BLOCK = 32
GROUPS = P // BLOCK
MOVES = GROUPS * GROUPS


def build(nc, x, qkv_w, qkv_b, proj_w, proj_b, w1, b1, w2, b2, out):
    x_halves = x.rearrange("b (u p t) c -> (b u) p (t c)", u=2, p=P)
    out_halves = out.rearrange("b (u p t) c -> (b u) p (t c)", u=2, p=P)

    ctx = ExitStack()
    with ctx:
        def sb(name, shape, dtype=F32):
            return ctx.enter_context(nc.sbuf_tensor(name, shape, dtype))

        def bank(name):
            return ctx.enter_context(nc.psum_tensor(name, [P, 512], F32))

        def sem(name):
            return ctx.enter_context(nc.semaphore(name))

        w1_hi, w1_lo = (sb(f"w1_{n}", [P, KC, INTER], F32R) for n in ("hi", "lo"))
        w2_hi, w2_lo = (sb(f"w2_{n}", [P, JC, C], F32R) for n in ("hi", "lo"))
        wqk_hi, wqk_lo = (sb(f"wqk_{n}", [P, KC, 2 * C], F32R) for n in ("hi", "lo"))
        wv_hi, wv_lo = (sb(f"wv_{n}", [P, KC, C], F32R) for n in ("hi", "lo"))
        proj_hi, proj_lo = (sb(f"proj_{n}", [P, KC, C], F32R) for n in ("hi", "lo"))
        bias_qk = sb("bias_qk", [P, 2 * C])
        bias_out = sb("bias_out", [P, C])
        bias_v = sb("bias_v", [P, KC])
        bias_h = sb("bias_h", [P, JC])
        ident = sb("ident", [P, P])
        ones = sb("ones", [P, P], F32R)
        head_mask = sb("head_mask", [P, KC, P])

        x_sb = sb("x_sb", [P, 2, TILES, C])
        y_sb = sb("y_sb", [P, 2, TILES, C])
        xn = sb("xn", [P, TILES, C])
        xn_hi, xn_lo = (sb(f"xn_{n}", [P, 2, TILES, C], F32R) for n in ("hi", "lo"))
        blocks = sb("blocks", [P, 2, C // BLOCK, BLOCK, TILES])
        x_blocks, q_blocks = blocks[:, 0], blocks[:, 1]
        xT_hi, xT_lo = (sb(f"xT_{n}", [P, 2, KC, HALF], F32R) for n in ("hi", "lo"))
        h_f32 = sb("h_f32", [P, HF_RING, HALF])
        h_hi, h_lo = (sb(f"h_{n}", [P, JC, HALF], F32R) for n in ("hi", "lo"))
        qk = sb("qk", [P, TILES, 2 * C])
        qk_sq = sb("qk_sq", [P, 2, 2 * C])
        k_hi, k_lo = (sb(f"k_{n}", [P, TILES, C], F32R) for n in ("hi", "lo"))
        qT_hi, qT_lo = (sb(f"qT_{n}", [P, KC, TOKENS], F32R) for n in ("hi", "lo"))
        k_sum = sb("k_sum", [P, C])
        ks_hi, ks_lo = (sb(f"ks_{n}", [P, C], F32R) for n in ("hi", "lo"))
        g_parts = sb("g_parts", [P, KC, 2, C], F32R)
        g_hi, g_lo = g_parts[:, :, 0, :], g_parts[:, :, 1, :]
        bv_ks = sb("bv_ks", [P, KC, P])
        kv = sb("kv", [P, KC, P])
        kv_hi, kv_lo = (sb(f"kv_{n}", [P, KC, P], F32R) for n in ("hi", "lo"))
        m_hi, m_lo = (sb(f"m_{n}", [P, KC, C], F32R) for n in ("hi", "lo"))
        ln_parts = sb("ln_parts", [P, TILES, 6])
        ln_sum, ln_dif, ln_m2, ln_mean = (sb(f"ln_{n}", [P, TILES]) for n in ("sum", "dif", "m2", "mean"))
        ln_v, ln_sd, ln_y0, ln_e, ln_rstd = (sb(f"ln_{n}", [P, TILES]) for n in ("v", "sd", "y0", "e", "rstd"))
        qk_v, qk_sd, qk_y0, qk_e, qk_rn = (sb(f"qk_{n}", [P, TILES, 2 * HEADS])
                                           for n in ("v", "sd", "y0", "e", "rn"))
        unread = sb("unread", [P, 1])
        bias_ffn, ones_f32 = k_sum, bv_ks[:, 0, :]
        wqk_raw = qk[:, 0:KC, :]
        w1_raw = h_f32[:].rearrange("p a b -> p (a b)").rearrange("p (k n) -> p k n", k=KC)
        w2_raw = blocks[:].rearrange("p w j c t -> p (w j c t)").rearrange("p (j n) -> p j n", j=JC)
        wv_raw, proj_raw = y_sb[:, 1, 0:KC, :], y_sb[:, 1, KC:2 * KC, :]

        w_bank = [bank(f"w_bank{k}") for k in range(2)]
        v_bank = [bank(f"v_bank{k}") for k in range(2)]
        o_bank = [bank(f"o_bank{k}") for k in range(2)]
        g_bank = bank("g_bank")
        kv_bank = bank("kv_bank")
        ks_all = v_bank[0][:, 0:C]
        kv_raw = kv_bank[:].rearrange("p (g w n) -> p g w n", g=KC, w=2)

        x_loaded = [sem(f"x_loaded{u}") for u in range(2)]
        x_first_loaded = sem("x_first_loaded")
        wqk_loaded, w1_loaded, w2_loaded, wvp_loaded = (sem(f"{n}_loaded") for n in ("wqk", "w1", "w2", "wvp"))
        bias_qk_loaded, bias_h_loaded, bias_v_loaded, bias_o_loaded = (
            sem(f"bias_{n}_loaded") for n in ("qk", "h", "v", "o"))
        stored = [sem(f"stored{u}") for u in range(2)]
        const_set = sem("const_set")
        ones_ready, bias_out_ready = sem("ones_ready"), sem("bias_out_ready")
        wqk_hi_ready, w1_hi_ready, w2_hi_ready = (sem(f"{n}_hi_ready") for n in ("wqk", "w1", "w2"))
        wqk_ready, w1_ready, w2_ready = (sem(f"{n}_ready") for n in ("wqk", "w1", "w2"))
        wvp_hi_ready, wvp_ready = sem("wvp_hi_ready"), sem("wvp_ready")
        ln_parts_done, ln_sums_done, ln_terms_done = (sem(f"ln_{n}_done") for n in ("parts", "sums", "terms"))
        ln_v_done, ln_sd_done, ln_y0_done, ln_e1_done, ln_e2_done, ln_rstd_done = (
            sem(f"ln_{n}_done") for n in ("v", "sd", "y0", "e1", "e2", "rstd"))
        xn_done, xn_hi_done, xn_split_done = sem("xn_done"), sem("xn_hi_done"), sem("xn_split_done")
        y_set = sem("y_set")
        x_transposed, x_moved, xT_ready = sem("x_transposed"), sem("x_moved"), sem("xT_ready")
        xT_hi_done, xT_lo_done = sem("xT_hi_done"), sem("xT_lo_done")
        qk_ready, qk_biased, qk_sq_done, qk_ss_done = (sem(f"qk_{n}") for n in ("ready", "biased", "sq_done", "ss_done"))
        qk_v_done, qk_sd_done, qk_y0_done, qk_e1_done, qk_e2_done, qk_rn_done = (
            sem(f"qk_{n}_done") for n in ("v", "sd", "y0", "e1", "e2", "rn"))
        k_done, q_done = sem("k_done"), sem("q_done")
        k_hi_done, k_lo_done, k_sum_step = (sem(n) for n in ("k_hi_done", "k_lo_done", "k_sum_step"))
        ks_hi_done, ks_done = sem("ks_hi_done"), sem("ks_done")
        g_done = sem("g_done")
        q_transposed, q_moved = sem("q_transposed"), sem("q_moved")
        qT_hi_done, qT_lo_done = sem("qT_hi_done"), sem("qT_lo_done")
        h_ready, h_done, h_hi_done, h_copied, h_lo_done = (
            sem(n) for n in ("h_ready", "h_done", "h_hi_done", "h_copied", "h_lo_done"))
        y_ready = sem("y_ready")
        y_done = sem("y_done")
        g_hi_done, g_lo_done, kv_ready, bv_ks_done = (sem(n) for n in ("g_hi_done", "g_lo_done", "kv_ready", "bv_ks_done"))
        kv_biased, kv_sum_done, kv_masked, kv_hi_done, kv_done = (
            sem(n) for n in ("kv_biased", "kv_sum_done", "kv_masked", "kv_hi_done", "kv_done"))
        m_ready, m_hi_done, m_lo_done = sem("m_ready"), sem("m_hi_done"), sem("m_lo_done")
        o_ready, o_done = sem("o_ready"), sem("o_done")

        def wait(eng, semaphore, count):
            if not (isinstance(count, int) and count <= 0):
                eng.wait_ge(semaphore, count)

        def by_tile(columns):
            return columns.rearrange("f (p t) -> f t p", t=TILES)

        def all_batches(eng, body):
            body(0, False)
            with eng.Fori(1, BATCHES - 1) as b:
                body(b, False)
            body(BATCHES - 1, True)

        block = ctx.enter_context(nc.Block())

        @block.sync
        def _(sp):
            for n, loaded in enumerate((x_first_loaded, x_loaded[0])):
                sp.dma_start(x_sb[:, 0, 2 * n:2 * n + 2, :], x_halves[0][:, 2 * n * C:2 * (n + 1) * C]).then_inc(loaded, 16)
            sp.dma_start(wqk_raw, qkv_w[:, 0:2 * C].rearrange("(k p) n -> p k n", p=P)).then_inc(wqk_loaded, 16)
            sp.dma_start(bias_qk[:], qkv_b[0:2 * C].partition_broadcast(P)).then_inc(bias_qk_loaded, 16)
            sp.dma_start(w1_raw, w1.rearrange("(k p) n -> p k n", p=P)).then_inc(w1_loaded, 16)
            sp.dma_start(x_sb[:, 1, :, :], x_halves[1]).then_inc(x_loaded[1], 16)
            sp.dma_start(bias_h[:], b1.rearrange("(j p) -> p j", p=P),
                         allow_slow_non_contiguous=True).then_inc(bias_h_loaded, 16)
            sp.dma_start(w2_raw, w2.rearrange("(j p) n -> p j n", p=P)).then_inc(w2_loaded, 16)
            sp.dma_start(bias_out[:], proj_b.partition_broadcast(P)).then_inc(bias_o_loaded, 16)
            sp.dma_start(bias_ffn[:], b2.partition_broadcast(P)).then_inc(bias_o_loaded, 16)
            sp.dma_start(bias_v[:], qkv_b[2 * C:3 * C].rearrange("(k p) -> p k", p=P),
                         allow_slow_non_contiguous=True).then_inc(bias_v_loaded, 16)
            sp.dma_start(wv_raw, qkv_w[:, 2 * C:3 * C].rearrange("(k p) n -> p k n", p=P)).then_inc(wvp_loaded, 16)
            sp.dma_start(proj_raw, proj_w.rearrange("(k p) n -> p k n", p=P)).then_inc(wvp_loaded, 16)

            def move(blocks, to, moved):
                by_chunk = blocks.rearrange("p (k j) c t -> p k j (c t)", k=KC)
                for a in range(GROUPS):
                    for j in range(GROUPS):
                        sp.dma_start(to[j * BLOCK:(j + 1) * BLOCK, :, a * P:(a + 1) * P].bitcast(F32),
                                     by_chunk[a * BLOCK:(a + 1) * BLOCK, :, j, :]).then_inc(moved, 16)

            def body(b, last):
                def load(u):
                    wait(sp, xn_done, 2 * b + u + 1)
                    wait(sp, y_set, 2 * b + u + 1)
                    sp.dma_start(x_sb[:, u, :, :].rearrange("p t c -> p (t c)"),
                                 x_halves[2 * b + u + 2]).then_inc(x_loaded[u], 16)

                if not last:
                    load(0)
                for u in range(2):
                    s = 2 * b + u
                    wait(sp, q_transposed, s + 1)
                    move(q_blocks, qT_lo[:, :, u * HALF:(u + 1) * HALF], q_moved)
                    if not last and u == 0:
                        load(1)
                    if not last:
                        wait(sp, x_transposed, s + 1)
                        wait(sp, g_done, s + 1)
                        move(x_blocks, xT_lo[:, u], x_moved)
                pieces = 2 if last else 1
                tiles = TILES // pieces
                for u in range(2):
                    for n in range(pieces):
                        wait(sp, o_done, 4 * b + 2 * u + 2 // pieces * (n + 1))
                        sp.dma_start(out_halves[2 * b + u][:, n * tiles * C:(n + 1) * tiles * C],
                                     y_sb[:, u, n * tiles:(n + 1) * tiles, :].rearrange("p t c -> p (t c)")
                                     ).then_inc(stored[u], 16)

            all_batches(sp, body)
            for u in range(2):
                sp.wait_ge(stored[u], 16 * (BATCHES + 1))

        @block.gpsimd
        def _(pool):
            def split_xn(s, u):
                wait(pool, g_done, s - 1)
                wait(pool, xn_hi_done, s + 1)
                nc.gpsimd.tensor_tensor(xn_lo[:, u], xn[:], xn_hi[:, u].bitcast(F32),
                                        ALU.subtract).then_inc(xn_split_done, 1)

            def set_y(b, u):
                wait(pool, x_loaded[u], 16 * (b + 1))
                wait(pool, stored[u], 16 * b)
                nc.gpsimd.tensor_tensor(y_sb[:, u], x_sb[:, u],
                                        bias_out[:].unsqueeze(1).to_broadcast([P, TILES, C]),
                                        ALU.add).then_inc(y_set, 1)

            def split_k(s):
                wait(pool, k_hi_done, s + 1)
                wait(pool, g_done, s)
                nc.gpsimd.tensor_tensor(k_lo[:], qk[:, :, C:2 * C], k_hi[:].bitcast(F32),
                                        ALU.subtract).then_inc(k_lo_done, 1)

            def sum_k(s, u):
                k = qk[:, :, C:2 * C]
                wait(pool, k_done, s + 1)
                if u == 0:
                    nc.gpsimd.tensor_tensor(k_sum[:], k[:, 0], k[:, 1], ALU.add).then_inc(k_sum_step, 2)
                    rest = range(2, TILES)
                else:
                    rest = range(TILES)
                for t in rest:
                    wait(pool, k_sum_step, TILES * s + t)
                    nc.gpsimd.tensor_tensor(k_sum[:], k_sum[:], k[:, t], ALU.add).then_inc(k_sum_step, 1)

            def split_k_sum(b):
                wait(pool, kv_ready, b)
                wait(pool, ks_hi_done, b + 1)
                nc.gpsimd.tensor_tensor(ks_lo[:], k_sum[:], ks_hi[:].bitcast(F32),
                                        ALU.subtract).then_inc(ks_done, 1)

            def qT_low(s, u):
                wait(pool, qT_hi_done, KC * (s + 1))
                half = (slice(None), slice(None), slice(u * HALF, (u + 1) * HALF))
                nc.gpsimd.tensor_tensor(qT_lo[half], qT_lo[half].bitcast(F32), qT_hi[half].bitcast(F32),
                                        ALU.subtract).then_inc(qT_lo_done, 1)

            nc.gpsimd.memset(ident[:], 0.0).then_inc(const_set, 1)
            nc.gpsimd.memset(ones_f32, 1.0).then_inc(const_set, 1)
            nc.gpsimd.memset(head_mask[:], 1.0).then_inc(const_set, 1)
            pool.wait_ge(const_set, 3)
            nc.gpsimd.affine_select(out=ident[:], in_=ident[:], compare_op=ALU.not_equal, fill=1.0, base=0,
                                    pattern=[[-1, P]], channel_multiplier=1).then_inc(const_set, 1)
            blocks = head_mask[:].rearrange("p g (n d) -> p (g n) d", d=D)
            heads_of_chunk = P // D
            for g in range(KC):
                part = blocks[:, g * heads_of_chunk:(g + 1) * heads_of_chunk, :]
                pool.wait_ge(const_set, 4 + 2 * g)
                nc.gpsimd.affine_select(out=part, in_=part, compare_op=ALU.is_ge, fill=0.0, base=0,
                                        pattern=[[-D, heads_of_chunk], [0, D]],
                                        channel_multiplier=1).then_inc(const_set, 1)
                pool.wait_ge(const_set, 5 + 2 * g)
                nc.gpsimd.affine_select(out=part, in_=part, compare_op=ALU.is_ge, fill=0.0, base=D - 1,
                                        pattern=[[D, heads_of_chunk], [0, D]],
                                        channel_multiplier=-1).then_inc(const_set, 1)
            pool.wait_ge(w1_hi_ready, 1)
            nc.gpsimd.tensor_tensor(w1_lo[:], w1_raw, w1_hi[:].bitcast(F32), ALU.subtract).then_inc(w1_ready, 1)
            split_xn(0, 0)
            pool.wait_ge(bias_o_loaded, 32)
            nc.gpsimd.tensor_tensor(bias_out[:], bias_out[:], bias_ffn[:], ALU.add).then_inc(bias_out_ready, 1)
            pool.wait_ge(w2_hi_ready, TILES)
            nc.gpsimd.tensor_tensor(w2_lo[:], w2_raw, w2_hi[:].bitcast(F32), ALU.subtract).then_inc(w2_ready, 1)
            pool.wait_ge(bias_out_ready, 1)
            set_y(0, 0)
            split_k(0)
            sum_k(0, 0)
            split_xn(1, 1)
            pool.wait_ge(wvp_loaded, 32)
            nc.gpsimd.tensor_copy(wv_hi[:], wv_raw).then_inc(wvp_hi_ready, 1)
            nc.gpsimd.tensor_copy(proj_hi[:], proj_raw).then_inc(wvp_hi_ready, 1)
            pool.wait_ge(wvp_hi_ready, 2)
            nc.gpsimd.tensor_tensor(wv_lo[:], wv_raw, wv_hi[:].bitcast(F32),
                                    ALU.subtract).then_inc(wvp_ready, 1)
            nc.gpsimd.tensor_tensor(proj_lo[:], proj_raw, proj_hi[:].bitcast(F32),
                                    ALU.subtract).then_inc(wvp_ready, 1)
            pool.wait_ge(wvp_ready, 2)
            set_y(0, 1)

            def body(b, last):
                s = 2 * b
                if not (isinstance(b, int) and b == 0):
                    split_k(s)
                    sum_k(s, 0)
                    set_y(b, 0)
                    set_y(b, 1)
                split_k(s + 1)
                sum_k(s + 1, 1)
                if not last:
                    split_xn(s + 2, 0)
                split_k_sum(b)
                qT_low(s, 0)
                if not last:
                    split_xn(s + 3, 1)
                qT_low(s + 1, 1)

            all_batches(pool, body)

        @block.scalar
        def _(act):
            def copy(to, what):
                return nc.scalar.activation(to, what, ACT.Copy)

            def ln_sqrt(s):
                wait(act, ln_v_done, s + 1)
                nc.scalar.activation(ln_sd[:], ln_v[:], ACT.Sqrt).then_inc(ln_sd_done, 1)

            def xn_high(s, u):
                wait(act, xn_done, s + 1)
                wait(act, g_done, s - 1)
                copy(xn_hi[:, u], xn[:]).then_inc(xn_hi_done, 1)

            def k_sum_high(b):
                wait(act, k_sum_step, 2 * TILES * (b + 1))
                wait(act, kv_ready, b)
                copy(ks_hi[:], k_sum[:]).then_inc(ks_hi_done, 1)

            def xT_high_first(s, u):
                for k in range(KC):
                    wait(act, xT_ready, KC * s + k + 1)
                    copy(by_tile(xT_hi[:, u, k, :]),
                         o_bank[k][:].rearrange("f (t p) -> f t p", t=TILES)).then_inc(xT_hi_done, 1)

            def xT_high(s, u):
                wait(act, x_moved, 16 * MOVES * (s - 1))
                for k in range(KC):
                    copy(xT_hi[:, u, k, :], xT_lo[:, u, k, :].bitcast(F32)).then_inc(xT_hi_done, 1)

            def qk_square(s, t):
                wait(act, qk_biased, TILES * s + t + 1)
                wait(act, qk_ss_done, TILES * s + t - 1)
                nc.scalar.activation(qk_sq[:, t % 2, :], qk[:, t, :], ACT.Square).then_inc(qk_sq_done, 1)

            def qk_sqrt(s):
                wait(act, qk_v_done, s + 1)
                nc.scalar.activation(qk_sd[:], qk_v[:], ACT.Sqrt).then_inc(qk_sd_done, 1)

            def k_high(s):
                wait(act, k_done, s + 1)
                wait(act, g_done, s)
                copy(k_hi[:], qk[:, :, C:2 * C]).then_inc(k_hi_done, 1)

            def h_chunk(s, j):
                wait(act, h_ready, JC * s + j + 1)
                if j == 0:
                    wait(act, y_ready, 2 * s)
                wait(act, h_lo_done, JC * s + j + 1 - HF_RING)
                nc.scalar.activation(h_f32[:, j % HF_RING, :], w_bank[j % 2][:], ACT.Relu,
                                     bias=bias_h[:, j:j + 1]).then_inc(h_done, 1)
                if j % 2 == 0:
                    wait(act, h_done, JC * s + j + 1)
                    copy(h_hi[:, j, :], h_f32[:, j % HF_RING, :]).then_inc(h_hi_done, 1)

            def qT_high(s, u):
                wait(act, q_moved, 16 * MOVES * (s + 1))
                for k in range(KC):
                    half = (slice(None), k, slice(u * HALF, (u + 1) * HALF))
                    copy(qT_hi[half], qT_lo[half].bitcast(F32)).then_inc(qT_hi_done, 1)

            act.wait_ge(const_set, 2)
            nc.scalar.activation(unread[:], ones_f32[:, 0:1], ACT.Sqrt)
            ln_sqrt(0)
            act.wait_ge(wqk_loaded, 16)
            copy(wqk_hi[:], wqk_raw).then_inc(wqk_hi_ready, 1)
            copy(ones[:], ones_f32).then_inc(ones_ready, 1)
            xT_high_first(0, 0)
            act.wait_ge(w1_loaded, 16)
            copy(w1_hi[:], w1_raw).then_inc(w1_hi_ready, 1)
            xn_high(0, 0)
            ln_sqrt(1)
            act.wait_ge(w2_loaded, 16)
            for t in range(TILES):
                qk_square(0, t)
                part = slice(t * JC // TILES, (t + 1) * JC // TILES)
                copy(w2_hi[:, part, :], w2_raw[:, part, :]).then_inc(w2_hi_ready, 1)
            act.wait_ge(bias_h_loaded, 16)
            act.wait_ge(bias_v_loaded, 16)

            def body(b, last):
                first = isinstance(b, int) and b == 0
                s = 2 * b
                if not first:
                    qk_sqrt(s)
                    xT_high(s + 1, 1)
                for j in range(JC):
                    h_chunk(s, j)
                    if j == 0 and first:
                        qk_sqrt(s)
                    if j == (4 if first else 1):
                        k_high(s)
                    if j == 6 and first:
                        xT_high_first(1, 1)
                if first:
                    xn_high(1, 1)
                for t in range(TILES):
                    qk_square(s + 1, t)
                qk_sqrt(s + 1)
                k_high(s + 1)
                if not last:
                    ln_sqrt(s + 2)
                for j in range(JC):
                    h_chunk(s + 1, j)
                    if j == 1:
                        k_sum_high(b)
                    if j == 3 and not last:
                        xn_high(s + 2, 0)
                wait(act, g_done, s + 2)
                copy(g_hi, g_bank[:].rearrange("p (k n) -> p k n", k=KC)).then_inc(g_hi_done, 1)
                qT_high(s, 0)
                if not last:
                    ln_sqrt(s + 3)
                    xT_high(s + 2, 0)
                    xn_high(s + 3, 1)
                wait(act, kv_ready, b + 1)
                wait(act, kv_sum_done, b)
                for g in range(KC):
                    done = nc.scalar.activation(bv_ks[:, g, :], ks_all[:, g * P:(g + 1) * P], ACT.Copy,
                                                scale=bias_v[:, g:g + 1])
                done.then_inc(bv_ks_done, 1)
                if last:
                    qT_high(s + 1, 1)
                wait(act, m_ready, b + 1)
                copy(m_hi[:], g_bank[:].rearrange("p (k n) -> p k n", k=KC)).then_inc(m_hi_done, 1)
                if not last:
                    qT_high(s + 1, 1)
                    for t in range(TILES):
                        qk_square(s + 2, t)

            all_batches(act, body)

        @block.vector
        def _(dve):
            def less(to, whole, high):
                return nc.vector.tensor_tensor(to, whole, high.bitcast(F32), ALU.subtract)

            def rsqrt(s, v, sd, y0, e, to, sd_done, y0_done, e1_done, e2_done, to_done):
                wait(dve, sd_done, s + 1)
                nc.vector.reciprocal(y0, sd).then_inc(y0_done, 1)
                wait(dve, y0_done, s + 1)
                nc.vector.tensor_tensor(e, v, y0, ALU.mult).then_inc(e1_done, 1)
                wait(dve, e1_done, s + 1)
                nc.vector.scalar_tensor_tensor(e, e, -0.5, y0, ALU.mult, ALU.mult).then_inc(e2_done, 1)
                wait(dve, e2_done, s + 1)
                nc.vector.scalar_tensor_tensor(to, e, 1.5, y0, ALU.add, ALU.mult).then_inc(to_done, 1)
                wait(dve, to_done, s + 1)

            def variance(s, b, u):
                first = isinstance(s, int) and s == 0
                if first:
                    wait(dve, x_first_loaded, 16)
                else:
                    wait(dve, x_loaded[u], 16 * (b + 1))
                for t in range(TILES):
                    if first and t == TILES // 2:
                        wait(dve, x_loaded[0], 16)
                    done = nc.vector.bn_stats(ln_parts[:, t, :], x_sb[:, u, t, :])
                done.then_inc(ln_parts_done, 1)
                wait(dve, ln_parts_done, s + 1)
                even, odd = ln_parts[:, :, 0:3], ln_parts[:, :, 3:6]
                nc.vector.tensor_tensor(ln_sum[:], even[:, :, 1], odd[:, :, 1], ALU.add)
                nc.vector.tensor_tensor(ln_dif[:], even[:, :, 1], odd[:, :, 1], ALU.subtract)
                nc.vector.tensor_tensor(ln_m2[:], even[:, :, 2], odd[:, :, 2], ALU.add).then_inc(ln_sums_done, 1)
                wait(dve, ln_sums_done, s + 1)
                nc.vector.tensor_scalar(ln_mean[:], ln_sum[:], 0.5, None, ALU.mult)
                nc.vector.tensor_scalar(ln_m2[:], ln_m2[:], 1.0 / C, LN_EPS, ALU.mult, ALU.add)
                nc.vector.scalar_tensor_tensor(ln_dif[:], ln_dif[:], 0.25, ln_dif[:], ALU.mult,
                                               ALU.mult).then_inc(ln_terms_done, 1)
                wait(dve, ln_terms_done, s + 1)
                nc.vector.tensor_tensor(ln_v[:], ln_m2[:], ln_dif[:], ALU.add).then_inc(ln_v_done, 1)
                wait(dve, ln_v_done, s + 1)

            def normalise(s, u):
                rsqrt(s, ln_v[:], ln_sd[:], ln_y0[:], ln_e[:], ln_rstd[:],
                      ln_sd_done, ln_y0_done, ln_e1_done, ln_e2_done, ln_rstd_done)
                if isinstance(s, int) and s <= 2:
                    wait(dve, xT_ready, KC * s)
                else:
                    wait(dve, x_transposed, s - 2)
                wait(dve, xn_split_done, s)
                for t in range(TILES):
                    done = nc.vector.tensor_scalar(xn[:, t, :], x_sb[:, u, t, :], ln_mean[:, t:t + 1],
                                                   ln_rstd[:, t:t + 1], ALU.subtract, ALU.mult)
                done.then_inc(xn_done, 1)

            def transpose_blocks(to, token_major, done):
                nc.vector.transpose(to.rearrange("p j c t -> p t j c"),
                                    token_major.rearrange("p t (j c) -> p t j c", c=BLOCK)).then_inc(done, 1)

            def transpose_x(s):
                wait(dve, xn_done, s + 1)
                wait(dve, x_moved, 16 * MOVES * (s - 2))
                transpose_blocks(x_blocks, xn[:], x_transposed)

            def transpose_q(s):
                wait(dve, q_done, s + 1)
                if isinstance(s, int) and s == 0:
                    wait(dve, w2_ready, 1)
                wait(dve, q_moved, 16 * MOVES * s)
                transpose_blocks(q_blocks, qk[:, :, 0:C], q_transposed)

            def xT_low_first(s, u):
                for k in range(KC):
                    wait(dve, xT_hi_done, KC * s + k + 1)
                    less(by_tile(xT_lo[:, u, k, :]), o_bank[k][:].rearrange("f (t p) -> f t p", t=TILES),
                         by_tile(xT_hi[:, u, k, :])).then_inc(xT_lo_done, 1)

            def xT_low(s, u, k):
                wait(dve, xT_hi_done, KC * s + k + 1)
                less(xT_lo[:, u, k, :], xT_lo[:, u, k, :].bitcast(F32), xT_hi[:, u, k, :]).then_inc(xT_lo_done, 1)

            def qk_sums(s, beside=lambda: None):
                def sums(t):
                    wait(dve, qk_sq_done, TILES * s + t + 1)
                    nc.vector.tensor_reduce(qk_v[:, t, :], qk_sq[:, t % 2, :].rearrange("p (h d) -> p h d", d=D),
                                            AXIS.X, ALU.add).then_inc(qk_ss_done, 1)

                wait(dve, q_transposed, s)
                wait(dve, k_lo_done, s)
                wait(dve, k_sum_step, TILES * s)
                for t in range(TILES):
                    wait(dve, qk_ready, TILES * s + t + 1)
                    nc.vector.tensor_tensor(qk[:, t, :], v_bank[t % 2][:], bias_qk[:], ALU.add).then_inc(qk_biased, 1)
                    if t == 1:
                        beside()
                    if t:
                        sums(t - 1)
                sums(TILES - 1)

            def bound(s):
                wait(dve, qk_ss_done, TILES * (s + 1))
                nc.vector.tensor_scalar(qk_v[:], qk_v[:], NORM_EPS * NORM_EPS, None, ALU.max).then_inc(qk_v_done, 1)

            def norms(s):
                wait(dve, qk_v_done, s + 1)
                rsqrt(s, qk_v[:], qk_sd[:], qk_y0[:], qk_e[:], qk_rn[:],
                      qk_sd_done, qk_y0_done, qk_e1_done, qk_e2_done, qk_rn_done)

            def divide(n, done):
                part = qk[:, :, n * C:(n + 1) * C].rearrange("p t (h d) -> p t h d", d=D)
                by = qk_rn[:, :, n * HEADS:(n + 1) * HEADS].unsqueeze(3).to_broadcast([P, TILES, HEADS, D])
                nc.vector.tensor_tensor(part, part, by, ALU.mult).then_inc(done, 1)

            def h_split(s, j):
                if j % 2 == 0:
                    wait(dve, h_hi_done, JC // 2 * s + j // 2 + 1)
                else:
                    wait(dve, h_done, JC * s + j + 1)
                    if j == 1:
                        wait(dve, y_ready, 2 * s)
                    nc.vector.tensor_copy(h_hi[:, j, :], h_f32[:, j % HF_RING, :]).then_inc(h_copied, 1)
                    wait(dve, h_copied, JC // 2 * s + j // 2 + 1)
                less(h_lo[:, j, :], h_f32[:, j % HF_RING, :], h_hi[:, j, :]).then_inc(h_lo_done, 1)

            def add_ffn(b, n):
                wait(dve, y_ready, 4 * b + n + 1)
                wait(dve, y_set, 2 * b + 1)
                tiles = y_sb[:, 0, 2 * n:2 * n + 2, :].rearrange("p t c -> p (t c)")
                nc.vector.tensor_tensor(tiles, o_bank[n][:], tiles, ALU.add).then_inc(y_done, 1)

            def add_attention(b, n):
                u, pair = n // 2, n % 2
                wait(dve, o_ready, 4 * b + n + 1)
                if u == 0:
                    wait(dve, y_done, 2 * b + n + 1)
                else:
                    wait(dve, y_set, 2 * b + 2)
                y = y_sb[:, u, 2 * pair:2 * pair + 2, :].rearrange("p t c -> p (t c)")
                nc.vector.tensor_tensor(y, (o_bank if u else w_bank)[pair][:], y, ALU.add).then_inc(o_done, 1)

            variance(0, 0, 0)
            normalise(0, 0)
            dve.wait_ge(wqk_hi_ready, 1)
            less(wqk_lo[:], wqk_raw, wqk_hi[:]).then_inc(wqk_ready, 1)
            xT_low_first(0, 0)
            variance(1, 0, 1)
            dve.wait_ge(bias_qk_loaded, 16)
            qk_sums(0)
            bound(0)
            normalise(1, 1)
            norms(0)

            def norm_ahead(s, b, u):
                variance(s, b, u)
                normalise(s, u)
                transpose_x(s)

            def body(b, last):
                first = isinstance(b, int) and b == 0
                s = 2 * b
                def last_chunks():
                    for j in range(JC - 2, JC):
                        h_split(s, j)

                for j in range(JC - 2):
                    h_split(s, j)
                    if j == 0 and first:
                        divide(1, k_done)
                    if j in (1, 3) and not first:
                        xT_low(s + 1, 1, j // 2)
                if first:
                    xT_low_first(1, 1)
                divide(0, q_done)
                if first:
                    transpose_q(s)
                    qk_sums(s + 1, last_chunks)
                else:
                    last_chunks()
                    transpose_q(s)
                    qk_sums(s + 1)
                bound(s + 1)
                norms(s + 1)
                divide(1, k_done)
                if not last:
                    norm_ahead(s + 2, b + 1, 0)
                add_ffn(b, 0)
                divide(0, q_done)
                transpose_q(s + 1)
                add_ffn(b, 1)
                for j in range(JC):
                    h_split(s + 1, j)
                wait(dve, g_hi_done, b + 1)
                less(g_lo, g_bank[:].rearrange("p (k n) -> p k n", k=KC), g_hi).then_inc(g_lo_done, 1)
                if not last:
                    norm_ahead(s + 3, b + 1, 1)
                    for k in range(KC):
                        xT_low(s + 2, 0, k)
                wait(dve, bv_ks_done, b + 1)
                nc.vector.tensor_tensor(kv[:], kv_raw[:, :, 0, :], bv_ks[:], ALU.add).then_inc(kv_biased, 1)
                wait(dve, kv_biased, b + 1)
                nc.vector.tensor_tensor(kv[:], kv_raw[:, :, 1, :], kv[:], ALU.add).then_inc(kv_sum_done, 1)
                wait(dve, kv_sum_done, b + 1)
                nc.vector.tensor_tensor(kv[:], kv[:], head_mask[:], ALU.mult).then_inc(kv_masked, 1)
                wait(dve, kv_masked, b + 1)
                nc.vector.tensor_copy(kv_hi[:], kv[:]).then_inc(kv_hi_done, 1)
                wait(dve, kv_hi_done, b + 1)
                less(kv_lo[:], kv[:], kv_hi[:]).then_inc(kv_done, 1)
                wait(dve, m_hi_done, b + 1)
                less(m_lo[:], g_bank[:].rearrange("p (k n) -> p k n", k=KC), m_hi[:]).then_inc(m_lo_done, 1)
                if not last:
                    qk_sums(s + 2)
                    bound(s + 2)
                add_attention(b, 0)
                add_attention(b, 1)
                if not last:
                    norms(s + 2)
                    divide(1, k_done)
                add_attention(b, 2)
                add_attention(b, 3)

            all_batches(dve, body)

        @block.tensor
        def _(pe):
            def product(to, left, right, first=True, last=True, shared=False):
                nc.tensor.matmul(to, left[0], right[0], start=first, stop=False, skip_group_check=shared)
                nc.tensor.matmul(to, left[0], right[1], start=False, stop=False, skip_group_check=shared)
                return nc.tensor.matmul(to, left[1], right[0], start=False, stop=last, skip_group_check=shared)

            def tile(t):
                return slice(t * P, (t + 1) * P)

            def of_tile(columns, t):
                return columns[:, t::TILES]

            def transpose_x(s):
                wait(pe, xn_done, s + 1)
                wait(pe, xT_lo_done, KC * s)
                for k in range(KC):
                    for t in range(TILES):
                        done = nc.tensor.transpose(o_bank[k][:, tile(t)], xn[:, t, k * P:(k + 1) * P], ident[:])
                    done.then_inc(xT_ready, 1)

            def query_key(s, u):
                wait(pe, xT_hi_done, KC * (s + 1))
                wait(pe, xT_lo_done, KC * (s + 1))
                for t in range(TILES):
                    wait(pe, qk_biased, TILES * s + t - 1)
                    for k in range(KC):
                        done = product(v_bank[t % 2][:],
                                       (of_tile(xT_hi[:, u, k, :], t), of_tile(xT_lo[:, u, k, :], t)),
                                       (wqk_hi[:, k, :], wqk_lo[:, k, :]), k == 0, k == KC - 1)
                    done.then_inc(qk_ready, 1)

            def ffn_up(s, batch, u, with_transposes=False):
                for j in range(JC):
                    if j < 2 and u == 0:
                        wait(pe, o_done, 4 * batch - 3 + j)
                    wait(pe, h_done, JC * s + j - 1)
                    for k in range(KC):
                        done = product(w_bank[j % 2][:],
                                       (w1_hi[:, k, tile(j)], w1_lo[:, k, tile(j)]),
                                       (xT_hi[:, u, k, :], xT_lo[:, u, k, :]), k == 0, k == KC - 1)
                    done.then_inc(h_ready, 1)
                    if j == JC - 2 and with_transposes:
                        transpose_x(s + 1)

            def gather(s, b, u):
                wait(pe, xn_split_done, s + 1)
                wait(pe, k_hi_done, s + 1)
                wait(pe, k_lo_done, s + 1)
                if u == 0:
                    wait(pe, m_lo_done, b)
                for t in range(TILES):
                    for k in range(KC):
                        done = product(g_bank[:, k * C:(k + 1) * C],
                                       (xn_hi[:, u, t, k * P:(k + 1) * P], xn_lo[:, u, t, k * P:(k + 1) * P]),
                                       (k_hi[:, t, :], k_lo[:, t, :]),
                                       u == 0 and t == 0 and k == 0, u == 1 and t == TILES - 1, shared=True)
                done.then_inc(g_done, 1)

            def ffn_down(s, u, t):
                to = o_bank[t // 2][:, (t % 2) * C:(t % 2 + 1) * C]
                for j in range(JC):
                    wait(pe, h_lo_done, JC * s + j + 1)
                    done = product(to, (of_tile(h_hi[:, j, :], t), of_tile(h_lo[:, j, :], t)),
                                   (w2_hi[:, j, :], w2_lo[:, j, :]),
                                   j == 0 and (u == 0 or t % 2 == 0), j == JC - 1 and u == 0, shared=u == 1)
                if t % 2:
                    done.then_inc(y_ready, 1)

            def key_value(b):
                wait(pe, ks_done, b + 1)
                wait(pe, g_lo_done, b + 1)
                wait(pe, kv_sum_done, b)
                nc.tensor.matmul(ks_all, ones[:], ks_hi[:], start=True, stop=False)
                nc.tensor.matmul(ks_all, ones[:], ks_lo[:], start=False, stop=True)
                for g in range(KC):
                    heads = slice(g * P, (g + 1) * P)
                    for k in range(KC):
                        nc.tensor.matmul(kv_raw[:, g, :, :], wv_hi[:, k, heads], g_parts[:, k, :, heads],
                                         start=g == 0 and k == 0, stop=False, skip_group_check=True)
                        done = nc.tensor.matmul(kv_raw[:, g, 0, :], wv_lo[:, k, heads], g_hi[:, k, heads],
                                                start=False, stop=g == KC - 1 and k == KC - 1, skip_group_check=True)
                done.then_inc(kv_ready, 1)

            def project(b):
                wait(pe, kv_done, b + 1)
                for g in range(KC):
                    done = product(g_bank[:, g * C:(g + 1) * C], (kv_hi[:, g, :], kv_lo[:, g, :]),
                                   (proj_hi[:, g, :], proj_lo[:, g, :]))
                done.then_inc(m_ready, 1)

            def attend(b):
                wait(pe, m_lo_done, b + 1)
                wait(pe, qT_lo_done, 2 * b + 1)
                wait(pe, h_done, JC * (2 * b + 2))
                for t in range(2 * TILES):
                    second = t >= TILES
                    if t == TILES:
                        wait(pe, qT_lo_done, 2 * b + 2)
                    half = slice(HALF, TOKENS) if second else slice(0, HALF)
                    bank_of = (o_bank if second else w_bank)[t % TILES // 2]
                    for g in range(KC):
                        done = product(bank_of[:, (t % 2) * C:(t % 2 + 1) * C],
                                       (of_tile(qT_hi[:, g, half], t % TILES), of_tile(qT_lo[:, g, half], t % TILES)),
                                       (m_hi[:, g, :], m_lo[:, g, :]),
                                       g == 0 and not second, g == KC - 1, shared=second)
                    if t % 2:
                        done.then_inc(o_ready, 1)

            def keep_warm(count):
                for _ in range(count):
                    nc.tensor.matmul(kv_bank[:, 0:P], ident[:], ident[:], start=True, stop=True)

            pe.wait_ge(const_set, 4)
            keep_warm(17)
            transpose_x(0)
            keep_warm(7)
            pe.wait_ge(wqk_ready, 1)
            query_key(0, 0)
            pe.wait_ge(w1_ready, 1)

            def body(b, last):
                first_half, second_half = 2 * b, 2 * b + 1
                first = isinstance(b, int) and b == 0
                ffn_up(first_half, b, 0, first)
                gather(first_half, b, 0)
                query_key(second_half, 1)
                if first:
                    pe.wait_ge(w2_ready, 1)
                for t in range(TILES):
                    if t % 2 == 0:
                        wait(pe, o_done, 4 * b - 1 + t // 2)
                    ffn_down(first_half, 0, t)
                ffn_up(second_half, b, 1)
                gather(second_half, b, 1)
                if first:
                    pe.wait_ge(wvp_ready, 2)
                    pe.wait_ge(ones_ready, 1)
                for t in range(TILES):
                    if t % 2 == 0:
                        wait(pe, y_done, 2 * b + t // 2 + 1)
                    ffn_down(second_half, 1, t)
                    if t == (0 if last else 1):
                        key_value(b)
                    if t == (2 if last else TILES - 1):
                        project(b)
                if not last:
                    query_key(second_half + 1, 0)
                attend(b)

            all_batches(pe, body)


INPUTS = {"L0_attn_x": "x", "L0_attn_qkv_w": "qkv_w", "L0_attn_qkv_b": "qkv_b", "L0_attn_proj_w": "proj_w",
          "L0_attn_proj_b": "proj_b", "L0_ffn_W1": "w1", "L0_ffn_b1": "b1", "L0_ffn_W2": "w2", "L0_ffn_b2": "b2"}


def kernel(**inputs):
    import concourse.bacc as bacc
    from concourse.bass_utils import run_bass_kernel_spmd

    nc = bacc.Bacc("TRN2", target_bir_lowering=False, num_devices=1)
    arrays, tensors = {}, {}
    for name, short in INPUTS.items():
        arrays[short] = np.ascontiguousarray(inputs[name])
        tensors[short] = nc.dram_tensor(short, arrays[short].shape, mybir.dt.from_np(arrays[short].dtype),
                                        kind="ExternalInput").ap()
    tensors["out"] = nc.dram_tensor("out", arrays["x"].shape, F32, kind="ExternalOutput").ap()
    build(nc, **tensors)
    return run_bass_kernel_spmd(nc, [arrays], core_ids=[0]).results[0]["out"]
```
